# Optimizing a Trainium2 kernel written in Bass

```python
import numpy as np
import jax
import jax.numpy as jnp

def _softmax(x, axis=-1):
    return jax.nn.softmax(x, axis=axis)

def _gelu(x):
    return jax.nn.gelu(x, approximate=True)

def _silu(x):
    return jax.nn.silu(x)

def _sigmoid(x):
    return jax.nn.sigmoid(x)

def _layernorm(x, axis=-1, eps=1e-05):
    m = jnp.mean(x, axis=axis, keepdims=True)
    v = jnp.var(x, axis=axis, keepdims=True)
    return (x - m) / jnp.sqrt(v + eps)

def _scatter_add(tgt, idx, src, axis=0):
    return tgt.at[idx].add(src)

def _segment_sum(src, seg, n):
    return jax.ops.segment_sum(src, seg, n)
kernel_name = 'mk_audio_tower_d1_tok_audfeat256_r4_fd8a9b'

def setup_inputs(seed: int=0):
    np.random.seed(seed)
    _w = jnp.asarray

    def _rec_inputs():
        import jax
        import jax.numpy as jnp
        _rk = jax.random.key(seed)
        x = 7.22013e-05 + 1.00017 * jax.random.normal(jax.random.fold_in(_rk, 1), (4, 750, 64), jnp.float32)
        return x
    x = _rec_inputs()

    def _L0_tok_setup():
        import jax, jax.numpy as jnp
        import numpy as np
        WIN = 9
        key = jax.random.key(seed)
        ks = jax.random.split(key, 4)
        N, L, C, U = (8, 1024, 64, 64)
        x = jax.random.normal(ks[0], (N, L, C), dtype=jnp.float32)
        W_qry = jax.random.normal(ks[1], (C, U), dtype=jnp.float32) * 0.05
        W_key = jax.random.normal(ks[2], (C, U), dtype=jnp.float32) * 0.05
        v = jax.random.normal(ks[3], (U,), dtype=jnp.float32) * 0.05
        b = jnp.zeros((U,), dtype=jnp.float32)
        return {'x': x, 'W_qry': W_qry, 'W_key': W_key, 'v': v, 'b': b}
    _L0_tok_all = _L0_tok_setup()
    _L0_tok_in = {k: v for k, v in _L0_tok_all.items() if k in ('W_qry', 'W_key', 'v', 'b')}
    del _L0_tok_all

    def _L0_attn_setup():
        import jax, jax.numpy as jnp
        import numpy as np
        SEQ_LEN = 512
        EMBED_DIM = 64
        BATCH = 8
        LN_EPS = 1e-05

        def _layernorm(x, g, b):
            mu = jnp.mean(x, axis=-1, keepdims=True)
            var = jnp.mean(jnp.square(x - mu), axis=-1, keepdims=True)
            return (x - mu) * jax.lax.rsqrt(var + LN_EPS) * g + b
        key = jax.random.key(seed)
        ks = jax.random.split(key, 8)
        C = EMBED_DIM
        x = jax.random.normal(ks[0], (BATCH, SEQ_LEN, C), dtype=jnp.float32)
        qkv_w = jax.random.normal(ks[1], (C, 3 * C), dtype=jnp.float32) * 0.02
        qkv_b = jnp.zeros((3 * C,), dtype=jnp.float32)
        proj_w = jax.random.normal(ks[2], (C, C), dtype=jnp.float32) * 0.02
        proj_b = jnp.zeros((C,), dtype=jnp.float32)
        ln1_g = jnp.ones((C,), dtype=jnp.float32)
        ln1_b = jnp.zeros((C,), dtype=jnp.float32)
        ln2_g = jnp.ones((C,), dtype=jnp.float32)
        ln2_b = jnp.zeros((C,), dtype=jnp.float32)
        bias_table = jax.random.truncated_normal(ks[3], -2.0, 2.0, (2 * SEQ_LEN - 1,), dtype=jnp.float32) * 0.02
        scale = jnp.asarray(1.0 / np.sqrt(C), dtype=jnp.float32)
        return {'x': x, 'ln1_g': ln1_g, 'ln1_b': ln1_b, 'qkv_w': qkv_w, 'qkv_b': qkv_b, 'bias_table': bias_table, 'scale': scale, 'proj_w': proj_w, 'proj_b': proj_b, 'ln2_g': ln2_g, 'ln2_b': ln2_b}
    _L0_attn_all = _L0_attn_setup()
    _L0_attn_in = {k: v for k, v in _L0_attn_all.items() if k in ('ln1_g', 'ln1_b', 'qkv_w', 'qkv_b', 'bias_table', 'scale', 'proj_w', 'proj_b', 'ln2_g', 'ln2_b')}
    del _L0_attn_all

    def _L0_ffn_setup():
        import jax, jax.numpy as jnp
        import numpy as np
        B, T, D, H, E = (16, 1024, 64, 128, 8)
        key = jax.random.key(seed)
        ks = jax.random.split(key, 5)
        x = jax.random.normal(ks[0], (B, T, D), dtype=jnp.float32)
        gate_w = jax.random.normal(ks[1], (D, E), dtype=jnp.float32) * 0.02
        gate_b = jnp.zeros((E,), dtype=jnp.float32)
        W1 = jax.random.normal(ks[2], (E, D, H), dtype=jnp.float32) * 0.02
        b1 = jnp.zeros((E, H), dtype=jnp.float32)
        W2 = jax.random.normal(ks[3], (E, H, D), dtype=jnp.float32) * 0.02
        b2 = jnp.zeros((E, D), dtype=jnp.float32)
        return {'x': x, 'gate_w': gate_w, 'gate_b': gate_b, 'W1': W1, 'b1': b1, 'W2': W2, 'b2': b2}
    _L0_ffn_all = _L0_ffn_setup()
    _L0_ffn_in = {k: v for k, v in _L0_ffn_all.items() if k in ('gate_w', 'gate_b', 'W1', 'b1', 'W2', 'b2')}
    del _L0_ffn_all
    return {'x': x, 'L0_tok_W_qry': _L0_tok_in['W_qry'], 'L0_tok_W_key': _L0_tok_in['W_key'], 'L0_tok_v': _L0_tok_in['v'], 'L0_tok_b': _L0_tok_in['b'], 'L0_attn_ln1_g': _L0_attn_in['ln1_g'], 'L0_attn_ln1_b': _L0_attn_in['ln1_b'], 'L0_attn_qkv_w': _L0_attn_in['qkv_w'], 'L0_attn_qkv_b': _L0_attn_in['qkv_b'], 'L0_attn_bias_table': _L0_attn_in['bias_table'], 'L0_attn_scale': _L0_attn_in['scale'], 'L0_attn_proj_w': _L0_attn_in['proj_w'], 'L0_attn_proj_b': _L0_attn_in['proj_b'], 'L0_attn_ln2_g': _L0_attn_in['ln2_g'], 'L0_attn_ln2_b': _L0_attn_in['ln2_b'], 'L0_ffn_gate_w': _L0_ffn_in['gate_w'], 'L0_ffn_gate_b': _L0_ffn_in['gate_b'], 'L0_ffn_W1': _L0_ffn_in['W1'], 'L0_ffn_b1': _L0_ffn_in['b1'], 'L0_ffn_W2': _L0_ffn_in['W2'], 'L0_ffn_b2': _L0_ffn_in['b2']}

def reference(x, L0_tok_W_qry, L0_tok_W_key, L0_tok_v, L0_tok_b, L0_attn_ln1_g, L0_attn_ln1_b, L0_attn_qkv_w, L0_attn_qkv_b, L0_attn_bias_table, L0_attn_scale, L0_attn_proj_w, L0_attn_proj_b, L0_attn_ln2_g, L0_attn_ln2_b, L0_ffn_gate_w, L0_ffn_gate_b, L0_ffn_W1, L0_ffn_b1, L0_ffn_W2, L0_ffn_b2):
    import jax
    import jax.numpy as jnp

    def _L0_tok_ref(x, W_qry, W_key, v, b):
        import jax, jax.numpy as jnp
        import numpy as np
        WIN = 9
        N, L, C = x.shape
        n_w = L - WIN + 1
        idx = jnp.arange(n_w)[:, None] + jnp.arange(WIN)[None, :]
        x_win = x[:, idx]
        x_ctr = x[:, WIN // 2:WIN // 2 + n_w]
        key = jnp.einsum('nwsc,cu->nwsu', x_win, W_key)
        qry = jnp.einsum('nwc,cu->nwu', x_ctr, W_qry)
        score = jnp.einsum('nwsu,u->nws', jnp.tanh(qry[:, :, None, :] + key + b), v)
        weight = jax.nn.softmax(score, axis=2)
        out = jnp.einsum('nwsc,nws->nwc', x_win, weight)
        return out

    def _L0_attn_ref(x, ln1_g, ln1_b, qkv_w, qkv_b, bias_table, scale, proj_w, proj_b, ln2_g, ln2_b):
        import jax, jax.numpy as jnp
        import numpy as np
        SEQ_LEN = 512
        EMBED_DIM = 64
        BATCH = 8
        LN_EPS = 1e-05

        def _layernorm(x, g, b):
            mu = jnp.mean(x, axis=-1, keepdims=True)
            var = jnp.mean(jnp.square(x - mu), axis=-1, keepdims=True)
            return (x - mu) * jax.lax.rsqrt(var + LN_EPS) * g + b
        B, N, C = x.shape
        h = _layernorm(x, ln1_g, ln1_b)
        qkv = h @ qkv_w + qkv_b
        q, k, v = jnp.split(qkv, 3, axis=-1)
        coords = jnp.arange(N)
        rel_idx = coords[None, :] - coords[:, None] + (N - 1)
        rel_bias = bias_table[rel_idx]
        attn = jnp.einsum('bnc,bmc->bnm', q, k) + rel_bias
        attn = jax.nn.softmax(attn, axis=-1) * scale
        out = jnp.einsum('bnm,bmc->bnc', attn, v)
        out = out @ proj_w + proj_b
        out = _layernorm(out, ln2_g, ln2_b)
        return out

    def _L0_ffn_ref(x, gate_w, gate_b, W1, b1, W2, b2):
        import jax, jax.numpy as jnp
        import numpy as np
        B, T, D, H, E = (16, 1024, 64, 128, 8)
        Bb, Tt, Dd = x.shape
        Ee = gate_w.shape[1]
        xf = x.reshape(-1, Dd)
        N = xf.shape[0]
        logits = xf @ gate_w + gate_b
        probs = jax.nn.softmax(logits, axis=-1)
        top2_vals, top2_idx = jax.lax.top_k(probs, 2)
        cw = jnp.zeros((N, Ee), dtype=xf.dtype).at[jnp.arange(N)[:, None], top2_idx].add(top2_vals)

        def step(acc, params):
            w1, bb1, w2, bb2, we = params
            h = jax.nn.gelu(xf @ w1 + bb1, approximate=False)
            y = h @ w2 + bb2
            return (acc + we[:, None] * y, None)
        out, _ = jax.lax.scan(step, jnp.zeros_like(xf), (W1, b1, W2, b2, cw.T))
        return out.reshape(Bb, Tt, Dd)
    h = _L0_tok_ref(x, L0_tok_W_qry, L0_tok_W_key, L0_tok_v, L0_tok_b)
    h = h + _L0_attn_ref(_layernorm(h, axis=-1), L0_attn_ln1_g, L0_attn_ln1_b, L0_attn_qkv_w, L0_attn_qkv_b, L0_attn_bias_table, L0_attn_scale, L0_attn_proj_w, L0_attn_proj_b, L0_attn_ln2_g, L0_attn_ln2_b)
    h = h + _L0_ffn_ref(_layernorm(h, axis=-1), L0_ffn_gate_w, L0_ffn_gate_b, L0_ffn_W1, L0_ffn_b1, L0_ffn_W2, L0_ffn_b2)
    return h

_drawn_inputs = setup_inputs


def setup_inputs(seed=0):
    import zlib

    import numpy as np

    out = dict(_drawn_inputs(seed))
    spreads = {'L0_tok_b': (0.0, 0.8),
     'L0_attn_ln1_g': (1.0, 0.6),
     'L0_attn_ln1_b': (0.0, 0.8),
     'L0_attn_qkv_b': (0.0, 0.41),
     'L0_attn_proj_b': (0.0, 0.1),
     'L0_attn_ln2_g': (1.0, 0.2),
     'L0_attn_ln2_b': (0.0, 0.1),
     'L0_ffn_gate_b': (0.0, 0.8),
     'L0_ffn_b1': (0.0, 0.8),
     'L0_ffn_b2': (0.0, 0.468)}
    factors = {'L0_tok_W_qry': 7.075,
     'L0_attn_qkv_w': 8.0,
     'L0_attn_bias_table': 8.0,
     'L0_attn_proj_w': 3.091,
     'L0_ffn_gate_w': 4.712,
     'L0_ffn_W1': 8.0,
     'L0_ffn_W2': 8.0}
    for name, (base, spread) in spreads.items():
        noise = np.random.default_rng([zlib.crc32(name.encode()), seed]).standard_normal(out[name].shape)
        drawn = base * np.exp(spread * noise) if base else spread * noise
        out[name] = jnp.asarray(drawn.astype(out[name].dtype))
    for name, factor in factors.items():
        out[name] = (out[name] * factor).astype(out[name].dtype)
    return out
```

```python
from contextlib import ExitStack

import concourse.bass as bass
from concourse import mybir

ALU = mybir.AluOpType
ACT = mybir.ActivationFunctionType
AX = mybir.AxisListType
F32 = mybir.dt.float32

B, L, C = 4, 750, 64
WIN = 9
NW = L - WIN + 1
P = 14 * WIN
NT = -(-NW // P)
NP = NT * P
HALF = NP // 2
TAIL = WIN - 1
GROUPS = NP // WIN + 1
TW = GROUPS * WIN
QKW = 776
H, E = 128, 8
EPS = 1e-5
BIG = 3.0e38
TABLE = 1023
LEAD = 2 * NW - 2 - (TABLE - 1)
ZW = (NT - 1) * P + NW
GROUPS_T = P // WIN + 1
EXT = ZW + P


def at_least(eng, sem, value):
    if isinstance(value, int) and value <= 0:
        return
    eng.wait_ge(sem, value)


def audio_tower(nc, x, w_qry, w_key, tok_v, tok_b, ln1_g, ln1_b, qkv_w, qkv_b, rtable, scale,
                proj_w, proj_b, ln2_g, ln2_b, gate_w, gate_b, w1, b1, w2, b2, out):
    with ExitStack() as ctx:
        def sb(name, shape):
            return ctx.enter_context(nc.sbuf_tensor(name, shape, F32))

        def sem(name):
            return ctx.enter_context(nc.semaphore(name))

        ps = ctx.enter_context(nc.psum_tensor("ps", [128, 8, 512], F32))
        table_ext = nc.dram_tensor("table_ext", (EXT,), F32)

        ident = sb("ident", [128, 128])
        band = sb("band", [P, GROUPS_T, WIN])
        rank = sb("rank", [P, E])
        half_neg = sb("half_neg", [P, NT])
        wk2 = sb("wk2", [128, 128])
        wq2 = sb("wq2", [128, 128])
        v2 = sb("v2", [128, 2])
        tokb = sb("tokb", [128, 1])
        g1c, b1c = sb("g1c", [C, 1]), sb("b1c", [C, 1])
        wqk = sb("wqk", [C, 2 * C])
        bqc, bkc = sb("bqc", [C, 1]), sb("bkc", [C, 1])
        wva = sb("wva", [C + 1, C])
        wvt = sb("wvt", [C, C + 1])
        wproj = sb("wproj", [C, C])
        wvp = sb("wvp", [C + 1, C])
        scalec = sb("scalec", [C + 1, 1])
        projb = sb("projb", [P, 1, C])
        g2b, b2b = sb("g2b", [P, 1, C]), sb("b2b", [P, 1, C])
        gatew = sb("gatew", [C, E])
        gateb = sb("gateb", [P, 1, E])
        w1s = sb("w1s", [C, E, H])
        b1s = sb("b1s", [H, E])
        w2s = sb("w2s", [H, E, C])
        b2s = sb("b2s", [E, C])
        hankel = sb("hankel", [P, ZW])

        xr = sb("xr", [128, 2, NT, 2, C])
        xT = sb("xT", [128, 2, NP])
        qbuf = sb("qbuf", [128, 2, QKW])
        kbuf = sb("kbuf", [128, 2, QKW])
        tt = sb("tt", [128, 2, WIN, TW])
        mx = sb("mx", [P, 2, 2 * NT])
        es = sb("es", [P, 2, 2 * NT, WIN])
        rs = sb("rs", [P, 2, 2 * NT])
        aw = sb("aw", [P, 2, 2 * NT, GROUPS_T * WIN])
        awT = sb("awT", [P, NT, P])
        awtT = sb("awtT", [TAIL, NT, P])
        h0 = sb("h0", [P, B, NT, C])

        st = sb("st", [P, NT, 6])
        ln = sb("ln", [P, 8, NT])
        n1 = sb("n1", [P, NT, C])

        hT = sb("hT", [C + 1, B, NP])
        kT = sb("kT", [C, B, NP])
        vp = sb("vp", [P, B, NT, C])
        qT = sb("qT", [C, NP])
        sc = sb("sc", [P, 2, NW])
        nmax = sb("nmax", [P, 2])
        pr = sb("pr", [P, 2, NP])
        rsum = sb("rsum", [P, NT])
        prT = sb("prT", [P, 2, NT, P])
        rinv = sb("rinv", [P, NT])
        ob = sb("ob", [P, NT, C])
        st2 = sb("st2", [P, NT, 6])
        ln2 = sb("ln2", [P, 8, NT])
        h1 = sb("h1", [P, B, NT, C])
        n3 = sb("n3", [P, NT, C])
        n3s = sb("n3s", [C, NP])
        n3T = sb("n3T", [C, B, NP])
        pt = sb("pt", [P, 6, NT, E])
        pm = sb("pm", [P, 4, NT])
        cws = sb("cws", [P, NT, E])
        cw = sb("cw", [P, B, NT, E])
        cwT = sb("cwT", [E, NP])

        gl = sb("gl", [H, 2, HALF])
        yw = aw[:, :, :, :].rearrange("p j t n -> p (j t n)")[:, 0:3 * E * C]\
            .rearrange("p (k e c) -> p k e c", k=3, c=C)
        ys = sb("ys", [P, 2, NT // 2, C])
        yo = h0

        x_in = [sem("x_in0"), sem("x_in1")]
        tokw_in, attw_in, ffnw_in = sem("tokw_in"), sem("attw_in"), sem("ffnw_in")
        ext_out, hankel_in = sem("ext_out"), sem("hankel_in")
        pad_set, blank_set, ident_set, const_set = (sem("pad_set"), sem("blank_set"), sem("ident_set"),
                                                    sem("const_set"))
        edge_set = sem("edge_set")
        mask_step = sem("mask_step")
        xT_mm, xT_ev, qk_mm, k_ev, q_ev = (sem("xT_mm"), sem("xT_ev"), sem("qk_mm"), sem("k_ev"),
                                           sem("q_ev"))
        sum_dve, sum_pool, tanh_done, f_mm = sem("sum_dve"), sem("sum_pool"), sem("tanh_done"), sem("f_mm")
        smax_chain, shifted, wexp, aw_done = (sem("smax_chain"), sem("shifted"), sem("wexp"),
                                              sem("aw_done"))
        awT_mm, awT_ev, awtT_ev, tok_mm = sem("awT_mm"), sem("awT_ev"), sem("awtT_ev"), sem("tok_mm")
        ln1_chain, ln1_var, ln1_pow, n1_done = (sem("ln1_chain"), sem("ln1_var"), sem("ln1_pow"),
                                                sem("n1_done"))
        hT_mm, hT_ev, kv_mm, kT_ev, vp_ev = sem("hT_mm"), sem("hT_ev"), sem("kv_mm"), sem("kT_ev"), sem("vp_ev")
        wv_mm, wv_ev = sem("wv_mm"), sem("wv_ev")
        q_mm, qT_ev, s_mm, s_max, p_done = sem("q_mm"), sem("qT_ev"), sem("s_mm"), sem("s_max"), sem("p_done")
        pT_mm, pT_ev_dve, pT_ev_act, pv_mm = sem("pT_mm"), sem("pT_ev_dve"), sem("pT_ev_act"), sem("pv_mm")
        o_chain, o_out = sem("o_chain"), sem("o_out")
        pool_chain, post_dve, o_bias, var2, h1_done, var3, n3_done = (
            sem("pool_chain"), sem("post_dve"), sem("o_bias"), sem("var2"), sem("h1_done"), sem("var3"),
            sem("n3_done"))
        post_mm, n3_ev, n3_copied, lg_shift, lg_exp, cw_done, cwT_ev, base_done = (
            sem("post_mm"), sem("n3_ev"), sem("n3_copied"), sem("lg_shift"), sem("lg_exp"), sem("cw_done"),
            sem("cwT_ev"), sem("base_done"))
        up_mm, gelu_done, down_mm, y_mul, y_red, y_sum = (sem("up_mm"), sem("gelu_done"), sem("down_mm"),
                                                          sem("y_mul"), sem("y_red"), sem("y_sum"))
        stored = sem("stored")

        X_DMA = 2 * 2 * 16
        REST = L - (NT - 1) * P
        FFNW = 9 * 16
        ATTW = 9 * 16
        block = ctx.enter_context(nc.Block())

        @block.sync
        def _(sp):
            def load_x(j):
                for hf in range(2):
                    b = 2 * j + hf
                    sp.dma_start(xr[0:P, j, 0:NT - 1, hf, :],
                                 x[b, 0:(NT - 1) * P, :].rearrange("(i p) c -> p i c", p=P)).then_inc(x_in[j], 16)
                    sp.dma_start(xr[0:REST, j, NT - 1, hf, :], x[b, (NT - 1) * P:L, :]).then_inc(x_in[j], 16)

            sp.wait_ge(pad_set, 1)
            load_x(0)
            sp.wait_ge(blank_set, 1)
            for hf in range(2):
                rows = slice(C * hf, C * hf + C)
                sp.dma_start(wk2[rows, rows], w_key).then_inc(tokw_in, 16)
                sp.dma_start(wq2[rows, rows], w_qry).then_inc(tokw_in, 16)
                sp.dma_start(v2[rows, hf:hf + 1], tok_v.rearrange("(c a) -> c a", a=1)).then_inc(tokw_in, 16)
                sp.dma_start(tokb[rows, :], tok_b.rearrange("(c a) -> c a", a=1)).then_inc(tokw_in, 16)
            load_x(1)
            sp.dma_start(bass.AP(table_ext, 0, [[1, LEAD], [1, 1]]),
                         bass.AP(rtable.tensor, 0, [[0, LEAD], [1, 1]])).then_inc(ext_out, 16)
            sp.dma_start(table_ext.ap()[LEAD:LEAD + TABLE], rtable).then_inc(ext_out, 16)
            rest = EXT - LEAD - TABLE
            sp.dma_start(table_ext.ap()[LEAD + TABLE:EXT], rtable[0:rest]).then_inc(ext_out, 16)
            for dst, src in ((g1c, ln1_g), (b1c, ln1_b), (bqc, qkv_b[0:C]), (bkc, qkv_b[C:2 * C])):
                sp.dma_start(dst[:, :], src.rearrange("(c a) -> c a", a=1)).then_inc(attw_in, 16)
            sp.dma_start(wqk[:, :], qkv_w[:, 0:2 * C]).then_inc(attw_in, 16)
            sp.dma_start(wva[0:C, :], qkv_w[:, 2 * C:3 * C]).then_inc(attw_in, 16)
            sp.dma_start(wva[C:C + 1, :], qkv_b[2 * C:3 * C].rearrange("(a c) -> a c", a=1)).then_inc(attw_in, 16)
            sp.dma_start(wproj[:, :], proj_w).then_inc(attw_in, 16)
            sp.dma_start(scalec[:, :], bass.AP(scale.tensor, 0, [[0, C + 1], [1, 1]])).then_inc(attw_in, 16)
            sp.wait_ge(ext_out, 48)
            sp.dma_start(hankel[:, :], bass.AP(table_ext, 0, [[1, P], [1, ZW]])).then_inc(hankel_in, 16)
            for dst, src, n in ((projb, proj_b, C), (g2b, ln2_g, C), (b2b, ln2_b, C), (gateb, gate_b, E)):
                sp.dma_start(dst[:, 0, :], bass.AP(src.tensor, 0, [[0, P], [1, n]])).then_inc(ffnw_in, 16)
            sp.dma_start(gatew[:, :], gate_w).then_inc(ffnw_in, 16)
            sp.dma_start(w1s[:, :, :], w1.rearrange("e c h -> c e h")).then_inc(ffnw_in, 16)
            sp.dma_start(b1s[:, :], b1).then_inc(ffnw_in, 16)
            sp.dma_start(w2s[:, :, :], w2.rearrange("e h c -> h e c")).then_inc(ffnw_in, 16)
            sp.dma_start(b2s[:, :], b2).then_inc(ffnw_in, 16)
            for b in range(B):
                sp.wait_ge(y_sum, 2 * (b + 1))
                sp.dma_start(out[b, 0:(NT - 1) * P, :].rearrange("(i p) c -> p i c", p=P),
                             yo[0:P, b, 0:NT - 1, :]).then_inc(stored, 16)
                sp.dma_start(out[b, (NT - 1) * P:NW, :], yo[0:NW - (NT - 1) * P, b, NT - 1, :]).then_inc(stored, 16)
            sp.wait_ge(stored, 32 * B)

        RD = 6

        def add_window(eng, j, r):
            q = qbuf[:, j, r:r + TW].rearrange("p (g i) -> p g i", i=WIN)
            k = kbuf[:, j, r:r + TW].rearrange("p (g i) -> p g i", i=WIN)[:, :, 0:1].to_broadcast([128, GROUPS, WIN])
            return eng.tensor_tensor(tt[:, j, r, :].rearrange("p (g i) -> p g i", i=WIN), q, k, ALU.add)

        @block.gpsimd
        def _(pool):
            nc.gpsimd.memset(wk2[:, :], 0.0)
            nc.gpsimd.memset(wq2[:, :], 0.0)
            nc.gpsimd.memset(v2[:, :], 0.0).then_inc(blank_set, 1)
            nc.gpsimd.memset(ident[:, :], 0.0).then_inc(mask_step, 1)
            nc.gpsimd.memset(band[:, :, :], 1.0).then_inc(mask_step, 1)
            pool.wait_ge(mask_step, 2)
            nc.gpsimd.affine_select(out=ident[:, :], in_=ident[:, :], compare_op=ALU.not_equal, fill=1.0, base=0,
                                    pattern=[[-1, 128]], channel_multiplier=1).then_inc(ident_set, 1)
            bandf = band[:, :, :].rearrange("p g r -> p (g r)")
            nc.gpsimd.affine_select(out=bandf, in_=bandf, compare_op=ALU.is_ge, fill=0.0, base=0,
                                    pattern=[[1, GROUPS_T * WIN]], channel_multiplier=-1).then_inc(mask_step, 1)
            pool.wait_ge(mask_step, 3)
            nc.gpsimd.affine_select(out=bandf, in_=bandf, compare_op=ALU.is_ge, fill=0.0, base=TAIL,
                                    pattern=[[-1, GROUPS_T * WIN]], channel_multiplier=1)
            for e in range(E):
                nc.gpsimd.memset(rank[:, e:e + 1], float(E - e))
            nc.gpsimd.memset(half_neg[:, :], -0.5).then_inc(const_set, 1)
            for j in range(2):
                pool.wait_ge(k_ev, j + 1)
                pool.wait_ge(q_ev, j + 1)
                for r in range(RD, WIN):
                    add_window(nc.gpsimd, j, r).then_inc(sum_pool, 1)
            pool.wait_ge(const_set, 1)
            for b in range(B):
                pool.wait_ge(ln1_var, b + 1)
                nc.gpsimd.tensor_tensor(ln[:, 5, :], ln[:, 4, :], half_neg[:, :], ALU.pow).then_inc(ln1_pow, 1)

            def post(b):
                k = [0]

                def link(ins):
                    k[0] += 1
                    ins.then_inc(pool_chain, 1)
                    pool.wait_ge(pool_chain, PN * b + k[0])

                def rows(t):
                    return t.unsqueeze(2).to_broadcast([P, NT, C])

                def cols(t):
                    return t[:, :, :].to_broadcast([P, NT, C])

                pool.wait_ge(o_out, b + 1)
                nc.gpsimd.tensor_tensor(ob[:, :, :], ob[:, :, :], cols(projb), ALU.add).then_inc(o_bias, 1)
                pool.wait_ge(var2, b + 1)
                link(nc.gpsimd.tensor_tensor(ln2[:, 5, :], ln2[:, 4, :], half_neg[:, :], ALU.pow))
                link(nc.gpsimd.tensor_tensor(ln2[:, 6, :], ln2[:, 0, :], ln2[:, 5, :], ALU.mult))
                link(nc.gpsimd.tensor_tensor(ob[:, :, :], ob[:, :, :], rows(ln2[:, 5, :]), ALU.mult))
                link(nc.gpsimd.tensor_tensor(ob[:, :, :], ob[:, :, :], rows(ln2[:, 6, :]), ALU.add))
                link(nc.gpsimd.tensor_tensor(ob[:, :, :], ob[:, :, :], cols(g2b), ALU.mult))
                link(nc.gpsimd.tensor_tensor(ob[:, :, :], ob[:, :, :], cols(b2b), ALU.add))
                hb = h1[:, bass.ds(b, 1), :, :].rearrange("p a i c -> p (a i) c")
                h0b = h0[:, bass.ds(b, 1), :, :].rearrange("p a i c -> p (a i) c")
                nc.gpsimd.tensor_tensor(hb, ob[:, :, :], h0b, ALU.add).then_inc(h1_done, 1)
                pool.wait_ge(var3, b + 1)
                at_least(pool, post_mm, 6 * (b - 1) + 2)
                link(nc.gpsimd.tensor_tensor(ln2[:, 5, :], ln2[:, 4, :], half_neg[:, :], ALU.pow))
                link(nc.gpsimd.tensor_tensor(ln2[:, 6, :], ln2[:, 0, :], ln2[:, 5, :], ALU.mult))
                link(nc.gpsimd.tensor_tensor(n3[:, :, :], hb, rows(ln2[:, 5, :]), ALU.mult))
                nc.gpsimd.tensor_tensor(n3[:, :, :], n3[:, :, :], rows(ln2[:, 6, :]), ALU.add).then_inc(n3_done, 1)
                pool.wait_ge(n3_ev, 2 * b + 2)
                nc.gpsimd.tensor_copy(n3T[:, bass.ds(b, 1), :].rearrange("c a n -> c (a n)"),
                                      n3s[:, :]).then_inc(n3_copied, 1)
                assert k[0] == PN

            PN = 9
            pool.wait_ge(ffnw_in, FFNW)
            post(0)
            for b in range(1, B):
                post(b)

            for b in range(B):
                for hf in range(2):
                    n = 2 * b + hf
                    tiles = slice(3 * hf, 3 * hf + 3)
                    pool.wait_ge(y_red, 3 * (n + 1))
                    if n == 0:
                        pool.wait_ge(base_done, B)
                    nc.gpsimd.tensor_tensor(yo[:, b, tiles, :], ys[:, n % 2, :, :], h1[:, b, tiles, :],
                                            ALU.add).then_inc(y_sum, 1)

        @block.vector
        def _(dve):
            nc.vector.memset(xr[96:128, :, NT - 1, :, :], 0.0).then_inc(pad_set, 1)
            for j in range(2):
                nc.vector.memset(qbuf[:, j, 0:4], 0.0)
                nc.vector.memset(qbuf[:, j, 4 + NP:QKW], 0.0)
                nc.vector.memset(kbuf[:, j, NP:QKW], 0.0)
            nc.vector.memset(pr[:, :, NW:NP], 0.0)
            nc.vector.memset(hT[C:C + 1, :, :], 1.0).then_inc(edge_set, 1)
            nc.vector.memset(nmax[:, :], 0.0).then_inc(smax_chain, 1)
            dve.wait_ge(smax_chain, 1)
            dve.wait_ge(tokw_in, 8 * 16)

            def queries(j):
                dve.wait_ge(qk_mm, j + 1)
                nc.vector.tensor_scalar(qbuf[:, j, 4:4 + NP].rearrange("p (h n) -> p h n", h=2),
                                        ps[:, 6:8, 0:HALF], tokb[:, 0:1], None, ALU.add).then_inc(q_ev, 1)

            def sums(j):
                dve.wait_ge(k_ev, j + 1)
                dve.wait_ge(q_ev, j + 1)
                for r in range(RD):
                    add_window(nc.vector, j, r).then_inc(sum_dve, 1)

            def window_softmax(j):
                f = ps[0:P, 2 * j, 0:2 * NT * WIN].rearrange("p (t r) -> p t r", r=WIN)
                dve.wait_ge(f_mm, j + 1)
                nc.vector.tensor_reduce(mx[:, j, :], f, AX.X, ALU.max).then_inc(smax_chain, 1)
                dve.wait_ge(smax_chain, 2 + 3 * j)
                nc.vector.tensor_tensor(es[:, j, :, :], f, mx[:, j, :].unsqueeze(2).to_broadcast([P, 2 * NT, WIN]),
                                        ALU.subtract).then_inc(shifted, 1)

            def window_weights(j):
                dve.wait_ge(wexp, j + 1)
                if j == 0:
                    dve.wait_ge(const_set, 1)
                nc.vector.tensor_tensor(
                    aw[:, j, :, :].rearrange("p t (g r) -> p t g r", r=WIN),
                    es[:, j, :, :].unsqueeze(2).to_broadcast([P, 2 * NT, GROUPS_T, WIN]),
                    band[:, :, :].unsqueeze(1).to_broadcast([P, 2 * NT, GROUPS_T, WIN]),
                    ALU.mult).then_inc(aw_done, 1)
                nc.vector.tensor_reduce(mx[:, j, :], es[:, j, :, :], AX.X, ALU.add).then_inc(smax_chain, 1)
                dve.wait_ge(smax_chain, 3 + 3 * j)
                nc.vector.reciprocal(rs[:, j, :], mx[:, j, :]).then_inc(smax_chain, 1)
                dve.wait_ge(smax_chain, 4 + 3 * j)

            lc = [0]

            def ln1_link(ins):
                lc[0] += 1
                ins.then_inc(ln1_chain, 1)
                dve.wait_ge(ln1_chain, lc[0])

            def row_moments(chain, src, stats, w, var_scale, eps):
                for i in range(NT):
                    ins = nc.vector.bn_stats(stats[:, i, :], src[:, i, :])
                chain(ins)
                nc.vector.tensor_tensor(w[:, 7, :], stats[:, :, 1], stats[:, :, 4], ALU.add)
                nc.vector.tensor_tensor(w[:, 2, :], stats[:, :, 2], stats[:, :, 5], ALU.add)
                chain(nc.vector.tensor_tensor(w[:, 1, :], stats[:, :, 1], stats[:, :, 4], ALU.subtract))
                chain(nc.vector.tensor_tensor(w[:, 3, :], w[:, 1, :], w[:, 1, :], ALU.mult))
                chain(nc.vector.scalar_tensor_tensor(out=w[:, 3, :], in0=w[:, 3, :], scalar=C / 4.0, in1=w[:, 2, :],
                                                     op0=ALU.mult, op1=ALU.add))
                chain(nc.vector.tensor_scalar(w[:, 0, :], w[:, 7, :], -0.5, None, ALU.mult))
                return nc.vector.tensor_scalar(w[:, 4, :], w[:, 3, :], var_scale, eps, ALU.mult, ALU.add)

            def weights_up(b):
                dve.wait_ge(awT_mm, b + 1)
                if b >= 1:
                    dve.wait_ge(tok_mm, b)
                nc.vector.tensor_copy(awT[:, :, :].rearrange("p (h i) n -> p h (i n)", h=2),
                                      ps[0:P, 4:6, 0:HALF]).then_inc(awT_ev, 1)

            def first_norm(b):
                j, hf = b // 2, b % 2
                dve.wait_ge(tok_mm, b + 1)
                o = ps[0:P, 1 + 2 * (b % 2), 0:NT * C].rearrange("p (i c) -> p i c", c=C)
                r = rs[:, j, :].rearrange("p (i h) -> p i h", h=2)[:, :, hf:hf + 1].to_broadcast([P, NT, C])
                ln1_link(nc.vector.tensor_tensor(h0[:, b, :, :], o, r, ALU.mult))
                row_moments(ln1_link, h0[:, b, :, :], st, ln, (1.0 + EPS) / C, EPS * EPS).then_inc(ln1_var, 1)
                dve.wait_ge(ln1_pow, b + 1)
                ln1_link(nc.vector.tensor_tensor(ln[:, 6, :], ln[:, 0, :], ln[:, 5, :], ALU.mult))
                if b >= 1:
                    dve.wait_ge(hT_mm, b)
                for i in range(NT):
                    ins = nc.vector.tensor_scalar(n1[:, i, :], h0[:, b, i, :], ln[:, 5, i:i + 1], ln[:, 6, i:i + 1],
                                                  ALU.mult, ALU.add)
                ins.then_inc(n1_done, 1)

            def values(b):
                dve.wait_ge(kv_mm, b + 1)
                nc.vector.tensor_copy(vp[:, b, :, :], ps[0:P, 0, 0:NT * C].rearrange("p (i c) -> p i c", c=C))\
                    .then_inc(vp_ev, 1)

            queries(0)
            sums(0)
            queries(1)
            sums(1)
            window_softmax(0)
            window_weights(0)
            window_softmax(1)
            window_weights(1)
            for b in range(B):
                weights_up(b)
                first_norm(b)
                values(b)

            dve.wait_ge(hankel_in, 16)
            dve.wait_ge(ffnw_in, FFNW)

            def scores(b, i):
                n = NT * b + i
                dve.wait_ge(s_mm, n + 1)
                at_least(dve, p_done, n - 1)
                z0 = P * i + NW - 1
                bias = bass.AP(hankel, z0, [[ZW, P], [-(NW // 2), 2], [-1, NW // 2]])
                nc.vector.tensor_tensor_reduce(
                    out=sc[:, i % 2, :].rearrange("p (h m) -> p h m", h=2),
                    in0=ps[0:P, 2 * (i % 2):2 * (i % 2) + 2, 0:NW // 2], in1=bias, scale=-1.0, scalar=BIG,
                    op0=ALU.add, op1=ALU.min, accum_out=nmax[:, i % 2:i % 2 + 1]).then_inc(s_max, 1)

            def probs_up(b, i):
                n = NT * b + i
                dve.wait_ge(pT_mm, n + 1)
                at_least(dve, pv_mm, n - 1)
                nc.vector.tensor_copy(prT[:, i % 2, 0:3, :].rearrange("p i n -> p (i n)"),
                                      ps[0:P, 4, 0:HALF]).then_inc(pT_ev_dve, 1)

            def attention_out(b):
                dve.wait_ge(p_done, NT * b + NT)
                nc.vector.reciprocal(rinv[:, :], rsum[:, :]).then_inc(o_chain, 1)
                dve.wait_ge(o_chain, b + 1)
                dve.wait_ge(pv_mm, NT * b + NT)
                at_least(dve, h1_done, b)
                nc.vector.tensor_tensor(ob[:, :, :], ps[0:P, 6, 0:NT * C].rearrange("p (i c) -> p i c", c=C),
                                        rinv[:, :].unsqueeze(2).to_broadcast([P, NT, C]), ALU.mult).then_inc(o_out, 1)

            DN = 27

            def post(b, part, k):
                def link(ins):
                    k[0] += 1
                    ins.then_inc(post_dve, 1)
                    dve.wait_ge(post_dve, DN * b + k[0])

                if part == 0:
                    dve.wait_ge(o_bias, b + 1)
                    row_moments(link, ob, st2, ln2, 1.0 / C, EPS).then_inc(var2, 1)
                if part == 1:
                    dve.wait_ge(h1_done, b + 1)
                    row_moments(link, h1[:, bass.ds(b, 1), :, :].rearrange("p a i c -> p (a i) c"), st2, ln2,
                                1.0 / C, EPS).then_inc(var3, 1)
                if part == 2:
                    def wide(t):
                        return t.unsqueeze(2).to_broadcast([P, NT, E])
                    lg, eq, p, s1, s2 = (pt[:, n, :, :] for n in range(5))
                    top = pm[:, 0, :]
                    dve.wait_ge(post_mm, 6 * b + 3)
                    link(nc.vector.tensor_tensor(lg, ps[0:P, 7, 0:NT * E].rearrange("p (i e) -> p i e", e=E),
                                                 gateb[:, :, :].to_broadcast([P, NT, E]), ALU.add))
                    link(nc.vector.tensor_reduce(top, lg, AX.X, ALU.max))
                    nc.vector.tensor_tensor(lg, lg, wide(top), ALU.subtract).then_inc(lg_shift, 1)
                    dve.wait_ge(lg_exp, b + 1)
                    link(nc.vector.tensor_reduce(pm[:, 1, :], lg, AX.X, ALU.add))
                    link(nc.vector.reciprocal(pm[:, 2, :], pm[:, 1, :]))
                    link(nc.vector.tensor_tensor(p, lg, wide(pm[:, 2, :]), ALU.mult))
                    rk = rank[:, :].unsqueeze(1).to_broadcast([P, NT, E])

                    def pick(src, sel):
                        link(nc.vector.tensor_reduce(top, src, AX.X, ALU.max))
                        link(nc.vector.tensor_tensor(eq, src, wide(top), ALU.is_equal))
                        link(nc.vector.tensor_tensor(eq, eq, rk, ALU.mult))
                        link(nc.vector.tensor_reduce(pm[:, 3, :], eq, AX.X, ALU.max))
                        link(nc.vector.tensor_tensor(sel, eq, wide(pm[:, 3, :]), ALU.is_equal))

                    pick(p, s1)
                    link(nc.vector.scalar_tensor_tensor(out=lg, in0=s1, scalar=-2.0, in1=p, op0=ALU.mult, op1=ALU.add))
                    pick(lg, s2)
                    link(nc.vector.tensor_tensor(s1, s1, s2, ALU.add))
                    nc.vector.tensor_tensor(cws[:, :, :], s1, p, ALU.mult).then_inc(cw_done, 1)
                    nc.vector.tensor_tensor(cw[:, bass.ds(b, 1), :, :].rearrange("p a i e -> p (a i) e"), s1, p,
                                            ALU.mult)
                if part == 3:
                    dve.wait_ge(post_mm, 6 * b + 6)
                    hb = h1[:, bass.ds(b, 1), :, :].rearrange("p a i c -> p (a i) c")
                    nc.vector.tensor_tensor(hb, ps[0:P, 7, 0:NT * C].rearrange("p (i c) -> p i c", c=C), hb,
                                            ALU.add).then_inc(base_done, 1)

            k = [0]

            def attend(b, peeled):
                dve.wait_ge(q_mm, b + 1)
                nc.vector.tensor_scalar(qT[:, :].rearrange("c (h n) -> c h n", h=2), ps[0:C, 4:6, 0:HALF],
                                        bqc[:, 0:1], None, ALU.add).then_inc(qT_ev, 1)
                k[0] = 0
                scores(b, 0)
                for i in range(NT):
                    if i + 1 < NT:
                        scores(b, i + 1)
                    probs_up(b, i)
                    if not peeled and i in POST_AT:
                        post(b - 1, POST_AT[i], k)
                attention_out(b)
                if not peeled:
                    post(b - 1, 2, k)
                    post(b - 1, 3, k)

            POST_AT = {0: 0, 3: 1}
            attend(0, True)
            for b in range(1, B):
                attend(b, False)
            k[0] = 0
            for part in range(4):
                post(B - 1, part, k)
            assert k[0] == DN, k[0]

            def weigh(b, hf):
                n = 2 * b + hf
                dve.wait_ge(down_mm, E * (n + 1))
                at_least(dve, y_sum, n - 1)
                for t in range(NT // 2):
                    w = cw[:, bass.ds(b, 1), 3 * hf + t, :].rearrange("p a e -> p (a e)")
                    nc.vector.tensor_tensor(yw[:, t, :, :],
                                            ps[0:P, 3 * hf + t, :].rearrange("p (e c) -> p e c", c=C),
                                            w.unsqueeze(2).to_broadcast([P, E, C]), ALU.mult).then_inc(y_mul, 1)
                    dve.wait_ge(y_mul, 3 * n + t + 1)
                    nc.vector.tensor_reduce(ys[:, hf, t, :], yw[:, t, :, :].rearrange("p e c -> p c e"),
                                            AX.X, ALU.add).then_inc(y_red, 1)

            weigh(0, 0)
            weigh(0, 1)
            for b in range(1, B):
                weigh(b, 0)
                weigh(b, 1)

        @block.scalar
        def _(act):
            def keys(j):
                act.wait_ge(xT_mm, j + 1)
                nc.scalar.activation(xT[:, j, :].rearrange("p (h n) -> p h n", h=2),
                                     ps[:, 2 * j:2 * j + 2, 0:HALF], ACT.Copy).then_inc(xT_ev, 1)
                act.wait_ge(qk_mm, j + 1)
                if j == 0:
                    act.wait_ge(smax_chain, 1)
                nc.scalar.activation(kbuf[:, j, 0:NP].rearrange("p (h n) -> p h n", h=2),
                                     ps[:, 4:6, 0:HALF], ACT.Copy).then_inc(k_ev, 1)

            def tanhs(j):
                for r in range(0, WIN, 3):
                    if r < RD:
                        act.wait_ge(sum_dve, RD * j + r + 3)
                    else:
                        act.wait_ge(sum_pool, (WIN - RD) * j + r - RD + 3)
                    nc.scalar.activation(tt[:, j, r:r + 3, :], tt[:, j, r:r + 3, :], ACT.Tanh).then_inc(tanh_done, 1)

            def window_exp(j):
                act.wait_ge(shifted, j + 1)
                nc.scalar.activation(es[:, j, :, :], es[:, j, :, :], ACT.Exp).then_inc(wexp, 1)

            keys(0)
            keys(1)
            tanhs(0)
            act.wait_ge(wv_mm, 1)
            nc.scalar.activation(wvt[:, :], ps[0:C, 2, 256:256 + C + 1], ACT.Copy).then_inc(wv_ev, 1)
            act.wait_ge(wv_mm, 2)
            act.wait_ge(attw_in, ATTW)
            nc.scalar.activation(wvp[:, :], ps[0:C + 1, 2, 384:384 + C], ACT.Copy,
                                 scale=scalec[:, 0:1]).then_inc(wv_ev, 1)
            tanhs(1)
            window_exp(0)
            window_exp(1)
            for b in range(B):
                act.wait_ge(awT_mm, b + 1)
                if b >= 1:
                    act.wait_ge(tok_mm, b)
                nc.scalar.activation(awtT[:, 0:3, :], ps[0:TAIL, 6, 0:HALF].rearrange("p (i n) -> p i n", n=P), ACT.Copy)
                nc.scalar.activation(awtT[:, 3:5, :], ps[0:TAIL, 7, 0:2 * P].rearrange("p (i n) -> p i n", n=P),
                                     ACT.Copy).then_inc(awtT_ev, 1)
                act.wait_ge(hT_mm, b + 1)
                nc.scalar.activation(hT[0:C, b, :].rearrange("c (h n) -> c h n", h=2), ps[0:C, 4:6, 0:HALF],
                                     ACT.Identity, scale=g1c[:, 0:1], bias=b1c[:, 0:1]).then_inc(hT_ev, 1)
                act.wait_ge(kv_mm, b + 1)
                nc.scalar.activation(kT[:, b, :].rearrange("c (h n) -> c h n", h=2), ps[0:C, 6:8, 0:HALF],
                                     ACT.Identity, bias=bkc[:, 0:1]).then_inc(kT_ev, 1)

            def probs(b, i):
                n = NT * b + i
                act.wait_ge(s_max, n + 1)
                at_least(act, pT_mm, n - 1)
                if i == 0:
                    at_least(act, o_chain, b)
                nc.scalar.activation(pr[:, i % 2, 0:NW], sc[:, i % 2, :], ACT.Exp, bias=nmax[:, i % 2:i % 2 + 1],
                                     scale=-1.0, accum_out=rsum[:, i:i + 1]).then_inc(p_done, 1)

            def probs_up(b, i):
                n = NT * b + i
                act.wait_ge(pT_mm, n + 1)
                at_least(act, pv_mm, n - 1)
                nc.scalar.activation(prT[:, i % 2, 3:6, :].rearrange("p i n -> p (i n)"),
                                     ps[0:P, 5, 0:HALF], ACT.Copy).then_inc(pT_ev_act, 1)

            def post(b):
                for h in range(2):
                    act.wait_ge(post_mm, 6 * b + h + 1)
                    nc.scalar.activation(n3s[:, HALF * h:HALF * h + HALF], ps[0:C, 7, 0:HALF],
                                         ACT.Copy).then_inc(n3_ev, 1)
                act.wait_ge(lg_shift, b + 1)
                nc.scalar.activation(pt[:, 0, :, :], pt[:, 0, :, :], ACT.Exp).then_inc(lg_exp, 1)
                for h in range(2):
                    act.wait_ge(post_mm, 6 * b + h + 4)
                    nc.scalar.activation(cwT[:, HALF * h:HALF * h + HALF], ps[0:E, 7, 0:HALF],
                                         ACT.Copy).then_inc(cwT_ev, 1)

            def attend(b, peeled):
                probs(b, 0)
                for i in range(NT):
                    if i + 1 < NT:
                        probs(b, i + 1)
                    probs_up(b, i)
                if not peeled:
                    post(b - 1)

            act.wait_ge(edge_set, 1)
            attend(0, True)
            nc.scalar.preload_act_table(ACT.Exp)
            for b in range(1, B):
                attend(b, False)
            post(B - 1)

            def gelus(b, hf):
                for e in range(E):
                    n = E * (2 * b + hf) + e
                    act.wait_ge(up_mm, n + 1)
                    at_least(act, down_mm, n - 1)
                    nc.scalar.activation(gl[:, e % 2, :], ps[:, 6 + e % 2, 0:HALF], ACT.Gelu,
                                         bias=b1s[:, e:e + 1]).then_inc(gelu_done, 1)

            nc.scalar.preload_act_table(ACT.Gelu)
            gelus(0, 0)
            gelus(0, 1)
            for b in range(1, B):
                gelus(b, 0)
                gelus(b, 1)

        @block.tensor
        def _(pe):
            mm, tp = nc.tensor.matmul, nc.tensor.transpose

            def x_up(j):
                pe.wait_ge(x_in[j], X_DMA)
                for i in range(NT):
                    ins = tp(ps[:, 2 * j + i // 3, P * (i % 3):P * (i % 3) + P],
                             xr[0:P, j, i, :, :].rearrange("p h c -> p (h c)"), ident[0:P, 0:P])
                ins.then_inc(xT_mm, 1)

            def keys_queries(j):
                pe.wait_ge(xT_ev, j + 1)
                if j == 1:
                    pe.wait_ge(k_ev, 1)
                    pe.wait_ge(q_ev, 1)
                for w, bank in ((wk2, 4), (wq2, 6)):
                    for h in range(2):
                        ins = mm(ps[:, bank + h, 0:HALF], w[:, :], xT[:, j, HALF * h:HALF * h + HALF],
                                 start=True, stop=True)
                ins.then_inc(qk_mm, 1)

            def window_scores(j):
                f = ps[0:P, 2 * j, 0:2 * NT * WIN].rearrange("p (i h r) -> p i h r", h=2, r=WIN)
                for r in range(WIN):
                    if r % 3 == 0:
                        pe.wait_ge(tanh_done, 3 * j + r // 3 + 1)
                    for i in range(NT):
                        c0 = P * i + TAIL - r
                        ins = mm(f[:, i, :, r], tt[:, j, r, c0:c0 + P], v2[:, :], start=True, stop=True)
                ins.then_inc(f_mm, 1)

            pe.wait_ge(ident_set, 1)
            x_up(0)
            pe.wait_ge(tokw_in, 8 * 16)
            keys_queries(0)
            x_up(1)
            keys_queries(1)
            pe.wait_ge(attw_in, ATTW)
            tp(ps[0:C, 2, 256:256 + C + 1], wva[:, :], ident[0:C + 1, 0:C + 1]).then_inc(wv_mm, 1)
            window_scores(0)
            pe.wait_ge(wv_ev, 1)
            mm(ps[0:C + 1, 2, 384:384 + C], wvt[:, :], wproj[:, :], start=True, stop=True).then_inc(wv_mm, 1)
            window_scores(1)

            for b in range(B):
                j, hf = b // 2, b % 2
                if b == 0:
                    pe.wait_ge(q_ev, 2)
                    pe.wait_ge(k_ev, 2)
                if b % 2 == 0:
                    pe.wait_ge(aw_done, j + 1)
                if b >= 1:
                    pe.wait_ge(hT_ev, b)
                    pe.wait_ge(kT_ev, b)
                for i in range(NT):
                    ins = tp(ps[0:P, 4 + i // 3, P * (i % 3):P * (i % 3) + P], aw[:, j, 2 * i + hf, 0:P],
                             ident[0:P, 0:P])
                for i in range(NT - 1):
                    ins = tp(ps[0:TAIL, 6 + i // 3, P * (i % 3):P * (i % 3) + P],
                             aw[:, j, 2 * i + hf, P:P + TAIL], ident[0:P, 0:P])
                ins.then_inc(awT_mm, 1)
                pe.wait_ge(awT_ev, b + 1)
                pe.wait_ge(awtT_ev, b + 1)
                if b == 1:
                    pe.wait_ge(wexp, 2)
                if b >= 2:
                    pe.wait_ge(ln1_var, b - 1)
                o = ps[0:P, 1 + 2 * (b % 2), 0:NT * C].rearrange("p (i c) -> p i c", c=C)
                for i in range(NT):
                    last = i == NT - 1
                    ins = mm(o[:, i, :], awT[:, i, :], xr[0:P, j, i, hf, :], start=True, stop=last)
                    if not last:
                        ins = mm(o[:, i, :], awtT[:, i, :], xr[0:TAIL, j, i + 1, hf, :], start=False, stop=True)
                ins.then_inc(tok_mm, 1)
                pe.wait_ge(n1_done, b + 1)
                for i in range(NT):
                    ins = tp(ps[0:C, 4 + i // 3, P * (i % 3):P * (i % 3) + P], n1[:, i, :], ident[0:P, 0:P])
                ins.then_inc(hT_mm, 1)
                pe.wait_ge(hT_ev, b + 1)
                for h in range(2):
                    mm(ps[0:C, 6 + h, 0:HALF], wqk[:, C:2 * C], hT[0:C, b, HALF * h:HALF * h + HALF],
                       start=True, stop=True)
                if b == 0:
                    pe.wait_ge(wv_ev, 2)
                    pe.wait_ge(edge_set, 1)
                    pe.wait_ge(shifted, 1)
                else:
                    pe.wait_ge(vp_ev, b)
                for i in range(NT):
                    ins = mm(ps[0:P, 0, C * i:C * i + C], hT[:, b, P * i:P * i + P], wvp[:, :], start=True, stop=True)
                ins.then_inc(kv_mm, 1)
            pe.wait_ge(kT_ev, B)
            pe.wait_ge(vp_ev, B)

            def scores(b, i):
                n = NT * b + i
                at_least(pe, s_max, n - 1)
                for h in range(2):
                    ins = mm(ps[0:P, 2 * (i % 2) + h, 0:NW // 2], qT[:, P * i:P * i + P],
                             kT[:, bass.ds(b, 1), NW // 2 * h:NW // 2 * h + NW // 2].rearrange("c a n -> c (a n)"),
                             start=True, stop=True)
                ins.then_inc(s_mm, 1)

            def probs_up(b, i):
                n = NT * b + i
                pe.wait_ge(p_done, n + 1)
                if i >= 1:
                    pe.wait_ge(pT_ev_dve, n)
                    pe.wait_ge(pT_ev_act, n)
                else:
                    pe.wait_ge(qT_ev, b + 1)
                for m in range(NT):
                    ins = tp(ps[0:P, 4 + m // 3, P * (m % 3):P * (m % 3) + P], pr[:, i % 2, P * m:P * m + P],
                             ident[0:P, 0:P])
                ins.then_inc(pT_mm, 1)

            def values(b, i):
                n = NT * b + i
                pe.wait_ge(pT_ev_dve, n + 1)
                pe.wait_ge(pT_ev_act, n + 1)
                if i == 0:
                    at_least(pe, o_out, b)
                for m in range(NT):
                    ins = mm(ps[0:P, 6, C * i:C * i + C], prT[:, i % 2, m, :],
                             vp[:, bass.ds(b, 1), m, :].rearrange("p a c -> p (a c)"),
                             start=(m == 0), stop=(m == NT - 1))
                ins.then_inc(pv_mm, 1)

            def post(b, step):
                if step < 2:
                    if step == 0:
                        pe.wait_ge(n3_done, b + 1)
                    else:
                        pe.wait_ge(n3_ev, 2 * b + 1)
                    for i in range(3):
                        ins = tp(ps[0:C, 7, P * i:P * i + P], n3[:, 3 * step + i, :], ident[0:P, 0:P])
                elif step == 2:
                    pe.wait_ge(n3_ev, 2 * b + 2)
                    for i in range(NT):
                        ins = mm(ps[0:P, 7, E * i:E * i + E], n3s[:, P * i:P * i + P], gatew[:, :],
                                 start=True, stop=True)
                elif step < 5:
                    if step == 3:
                        pe.wait_ge(cw_done, b + 1)
                    else:
                        pe.wait_ge(cwT_ev, 2 * b + 1)
                    for i in range(3):
                        ins = tp(ps[0:E, 7, P * i:P * i + P], cws[:, 3 * (step - 3) + i, :], ident[0:P, 0:P])
                else:
                    pe.wait_ge(cwT_ev, 2 * b + 2)
                    for i in range(NT):
                        ins = mm(ps[0:P, 7, C * i:C * i + C], cwT[:, P * i:P * i + P], b2s[:, :],
                                 start=True, stop=True)
                ins.then_inc(post_mm, 1)

            def attend(b, peeled):
                if not peeled:
                    pe.wait_ge(pT_ev_dve, NT * b)
                    pe.wait_ge(pT_ev_act, NT * b)
                for h in range(2):
                    ins = mm(ps[0:C, 4 + h, 0:HALF], wqk[:, 0:C],
                             hT[0:C, bass.ds(b, 1), HALF * h:HALF * h + HALF].rearrange("c a n -> c (a n)"),
                             start=True, stop=True)
                ins.then_inc(q_mm, 1)
                pe.wait_ge(qT_ev, b + 1)
                scores(b, 0)
                scores(b, 1)
                for i in range(NT):
                    probs_up(b, i)
                    if i + 2 < NT:
                        scores(b, i + 2)
                    values(b, i)
                if not peeled:
                    for step in range(6):
                        post(b - 1, step)

            attend(0, True)
            pe.wait_ge(ffnw_in, FFNW)
            for b in range(1, B):
                attend(b, False)
            for step in range(6):
                post(B - 1, step)

            def experts(b, hf):
                def down(e):
                    n = E * (2 * b + hf) + e
                    pe.wait_ge(gelu_done, n + 1)
                    if e == 0:
                        at_least(pe, y_mul, 3 * (2 * b + hf - 1))
                    for t in range(NT // 2):
                        ins = mm(ps[0:P, 3 * hf + t, C * e:C * e + C], gl[:, e % 2, P * t:P * t + P], w2s[:, e, :],
                                 start=True, stop=True)
                    ins.then_inc(down_mm, 1)
                for e in range(E):
                    n = E * (2 * b + hf) + e
                    at_least(pe, gelu_done, n - 1)
                    mm(ps[:, 6 + e % 2, 0:HALF], w1s[:, e, :],
                       n3T[:, bass.ds(b, 1), HALF * hf:HALF * hf + HALF].rearrange("c a n -> c (a n)"),
                       start=True, stop=True).then_inc(up_mm, 1)
                    if e >= 1:
                        down(e - 1)
                down(E - 1)

            pe.wait_ge(n3_copied, B)
            pe.wait_ge(base_done, B)
            experts(0, 0)
            experts(0, 1)
            for b in range(1, B):
                experts(b, 0)
                experts(b, 1)


_INS = ['x', 'L0_tok_W_qry', 'L0_tok_W_key', 'L0_tok_v', 'L0_tok_b', 'L0_attn_ln1_g', 'L0_attn_ln1_b',
        'L0_attn_qkv_w', 'L0_attn_qkv_b', 'L0_attn_bias_table', 'L0_attn_scale', 'L0_attn_proj_w',
        'L0_attn_proj_b', 'L0_attn_ln2_g', 'L0_attn_ln2_b', 'L0_ffn_gate_w', 'L0_ffn_gate_b', 'L0_ffn_W1',
        'L0_ffn_b1', 'L0_ffn_W2', 'L0_ffn_b2']


def kernel(**inputs):
    import numpy as _np
    import concourse.bacc as _bacc
    from concourse.bass_utils import run_bass_kernel_spmd as _run

    nc = _bacc.Bacc("TRN2", target_bir_lowering=False, num_devices=1)
    arrays, args = {}, []
    for name in _INS:
        a = _np.asarray(inputs[name])
        if name == 'L0_attn_bias_table':
            a = a[::-1]
        if name == 'L0_ffn_b1':
            a = a.T
        if name == 'L0_attn_scale':
            a = a.reshape(1, 1)
        a = _np.ascontiguousarray(a)
        arrays[f"in_{name}"] = a
        args.append(nc.dram_tensor(f"in_{name}", a.shape, mybir.dt.from_np(a.dtype), kind="ExternalInput").ap())
    args.append(nc.dram_tensor("out_0", (B, NW, C), F32, kind="ExternalOutput").ap())
    audio_tower(nc, *args)
    r = _run(nc, [arrays], core_ids=[0])
    return r.results[0]["out_0"]
```

```python
from contextlib import ExitStack

import concourse.bass as bass
from concourse import mybir

ALU = mybir.AluOpType
ACT = mybir.ActivationFunctionType
AX = mybir.AxisListType
F32 = mybir.dt.float32
F32R = mybir.dt.float32r

B, L, C = 4, 750, 64
WIN = 9
NW = L - WIN + 1
P = 14 * WIN
NT = -(-NW // P)
NP = NT * P
HALF = NP // 2
TAIL = WIN - 1
GROUPS = NP // WIN + 1
TW = GROUPS * WIN
QKW = 776
H, E = 128, 8
EPS = 1e-5
BIG = 3.0e38
TABLE = 1023
EDGE = 96
NE = P - EDGE
LO = 32
RC = 3
MH = NW // 2
LEAD = 2 * NW - 2 - (TABLE - 1)
ZW = (NT - 1) * P + NW
GROUPS_T = P // WIN + 1
EXT = ZW + P


def at_least(eng, sem, value):
    if isinstance(value, int) and value <= 0:
        return
    eng.wait_ge(sem, value)


def by_slot(*batches):
    slots = {}
    for b, parts in enumerate(batches):
        for part, slot in enumerate(parts):
            slots.setdefault(slot, []).append((b, part))
    return slots


def audio_tower(nc, xrow, xcol, w_qry, w_key, tok_v, tok_b, ln1_g, ln1_b, qkv_w, qkv_b, rtable, scale,
                proj_w, proj_b, ln2_g, ln2_b, gate_w, gate_b, w1, b1, w2, b2, out):
    with ExitStack() as ctx:
        def sb(name, shape, dt=F32):
            return ctx.enter_context(nc.sbuf_tensor(name, shape, dt))

        def sem(name):
            return ctx.enter_context(nc.semaphore(name))

        ps = ctx.enter_context(nc.psum_tensor("ps", [128, 8, 512], F32))
        table_ext = nc.dram_tensor("table_ext", (EXT,), F32)

        def f32(t):
            return t.bitcast(F32)

        ident = sb("ident", [128, 128])
        band = sb("band", [P, GROUPS_T, WIN])
        rank = sb("rank", [P, E])
        half_neg = sb("half_neg", [P, 2 * NT])
        wk2, wq2 = sb("wk2", [128, 128]), sb("wq2", [128, 128])
        v2 = sb("v2", [128, 2])
        v9 = sb("v9", [128, WIN, WIN, 2, 2], F32R)
        tokb = sb("tokb", [128, 1])
        gcol, bcol = sb("gcol", [128, 1]), sb("bcol", [128, 1])
        qkb = sb("qkb", [128, 2])
        qkc = sb("qkc", [128, 2])
        wqkv = sb("wqkv", [128, 3 * C])
        wqk = sb("wqk", [128, 2, 2, C])
        wqk_h, wqk_l = sb("wqk_h", [128, 2, 2 * C], F32R), sb("wqk_l", [128, 2, 2 * C], F32R)
        bvc, tvc = sb("bvc", [C, 1]), sb("tvc", [C, 1])
        wvt = sb("wvt", [C, C])
        wproj = sb("wproj", [C, C])
        wvp = sb("wvp", [128, C])
        wvp_h, wvp_l = sb("wvp_h", [128, C], F32R), sb("wvp_l", [128, C], F32R)
        scalec = sb("scalec", [128, 1])
        projb = sb("projb", [P, 1, C])
        g2b, b2b = sb("g2b", [P, 1, C]), sb("b2b", [P, 1, C])
        gatew = sb("gatew", [128, E])
        gate_h, gate_l = sb("gate_h", [128, E], F32R), sb("gate_l", [128, E], F32R)
        gateb = sb("gateb", [P, 1, E])
        w1s = sb("w1s", [128, E, H])
        w1_h, w1_l = sb("w1_h", [128, E, H], F32R), sb("w1_l", [128, E, H], F32R)
        b1s = sb("b1s", [H, E])
        w2s = sb("w2s", [H, E, C])
        w2_hl = sb("w2_hl", [H, E, 2, C], F32R)
        b2s = sb("b2s", [LO + E, C])
        b2_h, b2_l = sb("b2_h", [LO + E, C], F32R), sb("b2_l", [LO + E, C], F32R)
        picker = sb("picker", [LO + E, E, H], F32R)
        hankel = sb("hankel", [P, ZW])

        xr = sb("xr", [128, 2, NT, 2, C])
        xT = sb("xT", [128, 2, NP])
        qbuf, kbuf = sb("qbuf", [128, 2, QKW]), sb("kbuf", [128, 2, QKW])
        ts = sb("ts", [128, 2, RC, TW])
        th, tl = sb("th", [128, 2, RC, TW + 1], F32R), sb("tl", [128, 2, RC, TW + 1], F32R)
        frow = sb("frow", [4 * WIN, NP])
        mx = sb("mx", [P, 2, 2 * NT])
        es = sb("es", [P, 2, 2 * NT, WIN])
        rs = sb("rs", [P, 2, 2 * NT])
        aw = sb("aw", [P, 2 * NT, GROUPS_T * WIN])
        awT = sb("awT", [P, NT, P])
        awE = sb("awE", [TAIL, NT - 1, P])
        h0 = sb("h0", [P, B, NT, C])

        st = sb("st", [P, 2 * NT, 6])
        ln = sb("ln", [P, 8, 2 * NT])
        n1 = sb("n1", [P, 2, NT, 2, C])

        hS = sb("hS", [128, B, NP], F32R)
        kS = sb("kS", [128, B, NP], F32R)
        v_hl = sb("v_hl", [P, B, NT, 2, C], F32R)
        sc = sb("sc", [P, 2, NW])
        nmax = sb("nmax", [P, 2])
        pr = xT[0:P, :, :]
        rsum, rinv = sb("rsum", [P, NT]), sb("rinv", [P, NT])
        pT_h, pT_l = sb("pT_h", [P, 2, NP], F32R), sb("pT_l", [P, 2, NP], F32R)
        ob, ol = sb("ob", [P, 2, NT, C]), sb("ol", [P, 2, NT, C])
        st2 = sb("st2", [P, NT, 6])
        ln2, ln3 = sb("ln2", [P, 8, NT]), sb("ln3", [P, 8, NT])
        h1 = xr[0:P, :, :, :, :].rearrange("p j i h c -> p (j i h c)")\
            .rearrange("p (b i c) -> p b i c", b=B, c=C)
        n3 = n1[:, 0, :, :, :]
        pt = sb("pt", [P, 6, NT, E])
        pm = sb("pm", [P, 4, NT])
        cws = sb("cws", [P, NT, E])

        pick_f = sc[0:LO + E, :, :].rearrange("p a m -> p (a m)")[:, 0:E * H].rearrange("p (e h) -> p e h", e=E)

        nS = hS
        flat = "p a r n -> p (a r n)"
        ts_f, th_f, tl_f = ts.ap().rearrange(flat), th.ap().rearrange(flat), tl.ap().rearrange(flat)
        cwS = tl_f[0:LO + E, 0:B * NP]
        qH = th_f[:, 0:B * NP].rearrange("p (b n) -> p b n", b=B)
        qL = [(tl_f if b < 2 else th_f)[:, (B + b % 2) * NP:(B + b % 2 + 1) * NP] for b in range(B)]
        RG, RH = 3, 4
        ge = ts_f[:, 0:RG * HALF].rearrange("p (k n) -> p k n", k=RG)
        gw = ts_f[:, RG * HALF:2 * RG * HALF].rearrange("p (k n) -> p k n", k=RG)
        ysb = ts_f[:, 2 * RG * HALF:(2 * RG + 2) * HALF].rearrange("p (k n) -> p k n", k=2)
        gh = th_f[:, 0:RH * HALF].rearrange("p (k n) -> p k n", k=RH)
        gl = th_f[:, RH * HALF:2 * RH * HALF].rearrange("p (k n) -> p k n", k=RH)
        yo = h0
        HI_DVE = (2, 5)

        x_in = [sem("x_in0"), sem("x_in1")]
        xrow_in, tokw_in, attw_in, ffnw_in = sem("xrow_in"), sem("tokw_in"), sem("attw_in"), sem("ffnw_in")
        ext_out, hankel_in, stored = sem("ext_out"), sem("hankel_in"), sem("stored")
        pad_set, blank_set, ident_set, const_set, edge_set, mask_step, b2_blank = (
            sem("pad_set"), sem("blank_set"), sem("ident_set"), sem("const_set"), sem("edge_set"),
            sem("mask_step"), sem("b2_blank"))
        prep_dve, prep_mm, prep_act, prep_pool = sem("prep_dve"), sem("prep_mm"), sem("prep_act"), sem("prep_pool")
        qk_mm, k_ev, q_ev = sem("qk_mm"), sem("k_ev"), sem("q_ev")
        sum_dve, sum_pool, tanh_h, tanh_f, tl_dve, tl_pool, f_mm = (
            sem("sum_dve"), sem("sum_pool"), sem("tanh_h"), sem("tanh_f"), sem("tl_dve"), sem("tl_pool"),
            sem("f_mm"))
        smax_chain, shifted, wexp, aw_done = sem("smax_chain"), sem("shifted"), sem("wexp"), sem("aw_done")
        f_copied, fT_mm, h0_off, s2_pow, s3_pow, s2_done, v9_blank = (
            sem("f_copied"), sem("fT_mm"), sem("h0_off"), sem("s2_pow"), sem("s3_pow"), sem("s2_done"),
            sem("v9_blank"))
        awT_mm, awT_ev, tok_mm, ln1_chain, h0_out, ln1_var, ln1_pow, n1_done = (
            sem("awT_mm"), sem("awT_ev"), sem("tok_mm"), sem("ln1_chain"), sem("h0_out"), sem("ln1_var"),
            sem("ln1_pow"), sem("n1_done"))
        hT_mm, hS_h, hS_l, k_mm, kS_h, kS_l, v_mm, v_h, v_l = (
            sem("hT_mm"), sem("hS_h"), sem("hS_l"), sem("k_mm"), sem("kS_h"), sem("kS_l"), sem("v_mm"),
            sem("v_h"), sem("v_l"))
        q_mm, q_h, q_l, s_mm, s_max, p_done = (sem("q_mm"), sem("q_h"), sem("q_l"), sem("s_mm"),
                                               sem("s_max"), sem("p_done"))
        pT_mm, pT_hi, pT_lo, pv_mm = sem("pT_mm"), sem("pT_hi"), sem("pT_lo"), sem("pv_mm")
        rinv_done, o_read, o_bias, var2, h1_done, var3, n3_done = (
            sem("rinv_done"), sem("o_read"), sem("o_bias"), sem("var2"), sem("h1_done"), sem("var3"),
            sem("n3_done"))
        pool_chain, post_dve, post_mm, nS_h, nS_l, lg_shift, lg_exp, cw_done, cw_h, cw_l, base_done = (
            sem("pool_chain"), sem("post_dve"), sem("post_mm"), sem("nS_h"), sem("nS_l"), sem("lg_shift"),
            sem("lg_exp"), sem("cw_done"), sem("cw_h"), sem("cw_l"), sem("base_done"))
        up_mm, cb_mm, gelu_done, gw_done, gh_act, gh_dve, gl_pool, gl_dve, down_mm = (
            sem("up_mm"), sem("cb_mm"), sem("gelu_done"), sem("gw_done"), sem("gh_act"), sem("gh_dve"),
            sem("gl_pool"), sem("gl_dve"), sem("down_mm"))
        y_copied, yT_mm, y_add, y_sum = sem("y_copied"), sem("yT_mm"), sem("y_add"), sem("y_sum")

        TOKW, ATTW, FFNW = 8 * 16, 12 * 16, 13 * 16
        REST = L - (NT - 1) * P
        KCH = 2 * (WIN // RC)
        KC = 2 * B * E
        block = ctx.enter_context(nc.Block())

        S0 = B * NT
        PE_POST = by_slot((11, 12, 13, 17, 18, 19), (20, 21, 22, S0 + 4, S0 + 6, S0 + 8),
                          (S0 + 10, S0 + 12, S0 + 14, S0 + 22, S0 + 24, S0 + 26),
                          (S0 + 28, S0 + 30, S0 + 32, S0 + 38, S0 + 40, S0 + 42))
        ACT_POST = by_slot((8, 10, 11, 12, 14, 17, 18), (14, 16, 20, 21, 23, S0 + 4, S0 + 6),
                           (20, 23, S0 + 10, S0 + 12, S0 + 16, S0 + 22, S0 + 24),
                           (S0 + 8, S0 + 18, S0 + 28, S0 + 30, S0 + 34, S0 + 38, S0 + 40))
        DVE_POST = by_slot((7, 9, 12, 13, 14, 15, 16, 18, 19, 20),
                           (13, 15, 21, 22, 23, S0, S0 + 2, S0 + 4, S0 + 6, S0 + 9),
                           (19, 22, S0 + 10, S0 + 12, S0 + 15, S0 + 17, S0 + 19, S0 + 22, S0 + 24, S0 + 27),
                           (S0 + 4, S0 + 13, S0 + 28, S0 + 30, S0 + 33, S0 + 35, S0 + 37, S0 + 38, S0 + 40, S0 + 43))
        POOL_POST = by_slot((), (), (), (S0 + 1, S0 + 6, S0 + 9, S0 + 15))

        def halves(bank, rows=128):
            return ps[0:rows, bank:bank + 2, 0:HALF]

        def cols(t):
            return t.rearrange("p (h n) -> p h n", h=2)

        def n_dve(k):
            return k // E * len(HI_DVE) + sum(e < k % E for e in HI_DVE)

        @block.sync
        def _(sp):
            def col(t):
                return t.rearrange("(c a) -> c a", a=1)

            sp.wait_ge(pad_set, 1)
            sp.dma_start(xT[:, 0, 0:L], xcol[0]).then_inc(x_in[0], 16)
            sp.wait_ge(blank_set, 1)
            for hf in range(2):
                rows = slice(C * hf, C * hf + C)
                sp.dma_start(wk2[rows, rows], w_key).then_inc(tokw_in, 16)
                sp.dma_start(wq2[rows, rows], w_qry).then_inc(tokw_in, 16)
                sp.dma_start(tokb[rows, :], col(tok_b)).then_inc(tokw_in, 16)
                sp.dma_start(v2[rows, hf:hf + 1], col(tok_v)).then_inc(tokw_in, 16)
            sp.dma_start(xT[:, 1, 0:L], xcol[1]).then_inc(x_in[1], 16)
            for hf in range(2):
                rows = slice(C * hf, C * hf + C)
                sp.dma_start(gcol[rows, :], col(ln1_g)).then_inc(attw_in, 16)
                sp.dma_start(bcol[rows, :], col(ln1_b)).then_inc(attw_in, 16)
                for n in range(2):
                    sp.dma_start(qkb[rows, n:n + 1], col(qkv_b[C * n:C * n + C])).then_inc(attw_in, 16)
                sp.dma_start(wqkv[rows, :], qkv_w).then_inc(attw_in, 16)
            sp.dma_start(bvc[:, :], col(qkv_b[2 * C:3 * C])).then_inc(attw_in, 16)
            sp.dma_start(wproj[:, :], proj_w).then_inc(attw_in, 16)
            sp.wait_ge(pad_set, 2)
            for b in range(B):
                j, hf = b // 2, b % 2
                sp.dma_start(xr[0:P, j, 0:NT - 1, hf, :],
                             xrow[b, 0:(NT - 1) * P, :].rearrange("(i p) c -> p i c", p=P)).then_inc(xrow_in, 16)
                sp.dma_start(xr[0:REST, j, NT - 1, hf, :], xrow[b, (NT - 1) * P:L, :]).then_inc(xrow_in, 16)
            sp.dma_start(scalec[:, :], bass.AP(scale.tensor, 0, [[0, 128], [1, 1]])).then_inc(ffnw_in, 16)
            sp.dma_start(bass.AP(table_ext, 0, [[1, LEAD], [1, 1]]),
                         bass.AP(rtable.tensor, 0, [[0, LEAD], [1, 1]])).then_inc(ext_out, 16)
            sp.dma_start(table_ext.ap()[LEAD:LEAD + TABLE], rtable).then_inc(ext_out, 16)
            rest = EXT - LEAD - TABLE
            sp.dma_start(table_ext.ap()[LEAD + TABLE:EXT], rtable[0:rest]).then_inc(ext_out, 16)
            for dst, src, n in ((projb, proj_b, C), (g2b, ln2_g, C), (b2b, ln2_b, C), (gateb, gate_b, E)):
                sp.dma_start(dst[:, 0, :], bass.AP(src.tensor, 0, [[0, P], [1, n]])).then_inc(ffnw_in, 16)
            sp.wait_ge(ext_out, 48)
            sp.dma_start(hankel[:, :], bass.AP(table_ext, 0, [[1, P], [1, ZW]])).then_inc(hankel_in, 16)
            for hf in range(2):
                rows = slice(C * hf, C * hf + C)
                sp.dma_start(gatew[rows, :], gate_w).then_inc(ffnw_in, 16)
                sp.dma_start(w1s[rows, :, :], w1.rearrange("e c h -> c e h")).then_inc(ffnw_in, 16)
            sp.dma_start(b1s[:, :], b1).then_inc(ffnw_in, 16)
            sp.dma_start(w2s[:, :, :], w2.rearrange("e h c -> h e c")).then_inc(ffnw_in, 16)
            sp.wait_ge(b2_blank, 1)
            for r0 in (0, LO):
                sp.dma_start(b2s[r0:r0 + E, :], b2).then_inc(ffnw_in, 16)
            for b in range(B):
                sp.wait_ge(y_sum, 2 * (b + 1))
                sp.dma_start(out[b, 0:(NT - 1) * P, :].rearrange("(i p) c -> p i c", p=P),
                             yo[0:P, b, 0:NT - 1, :]).then_inc(stored, 16)
                sp.dma_start(out[b, (NT - 1) * P:NW, :], yo[0:NW - (NT - 1) * P, b, NT - 1, :]).then_inc(stored, 16)
            sp.wait_ge(stored, 32 * B)

        def add_window(eng, k, r):
            j, res = k // (WIN // RC), RC * (k % (WIN // RC)) + r
            q = qbuf[:, j, res:res + TW].rearrange("p (g i) -> p g i", i=WIN)
            key = kbuf[:, j, res:res + TW].rearrange("p (g i) -> p g i", i=WIN)[:, :, 0:1]
            return eng.tensor_tensor(ts[:, k % 2, r, :].rearrange("p (g i) -> p g i", i=WIN), q,
                                     key.to_broadcast([128, GROUPS, WIN]), ALU.add)

        def low_part(eng, k, r):
            return eng.tensor_tensor(tl[:, k % 2, r, 0:TW], ts[:, k % 2, r, :], f32(th[:, k % 2, r, 0:TW]),
                                     ALU.subtract)

        RP = RC - 1

        @block.gpsimd
        def _(pool):
            nc.gpsimd.memset(wk2[:, :], 0.0)
            nc.gpsimd.memset(wq2[:, :], 0.0)
            nc.gpsimd.memset(v2[:, :], 0.0).then_inc(blank_set, 1)
            nc.gpsimd.memset(ident[:, :], 0.0).then_inc(mask_step, 1)
            nc.gpsimd.memset(band[:, :, :], 1.0).then_inc(mask_step, 1)
            nc.gpsimd.memset(pick_f, 0.0).then_inc(mask_step, 1)
            pool.wait_ge(mask_step, 3)
            nc.gpsimd.affine_select(out=ident[:, :], in_=ident[:, :], compare_op=ALU.not_equal, fill=1.0, base=0,
                                    pattern=[[-1, 128]], channel_multiplier=1).then_inc(ident_set, 1)
            bandf = band[:, :, :].rearrange("p g r -> p (g r)")
            nc.gpsimd.affine_select(out=bandf, in_=bandf, compare_op=ALU.is_ge, fill=0.0, base=0,
                                    pattern=[[1, GROUPS_T * WIN]], channel_multiplier=-1)
            nc.gpsimd.affine_select(out=pick_f, in_=pick_f, compare_op=ALU.not_equal, fill=1.0, base=0,
                                    pattern=[[-1, E], [0, H]], channel_multiplier=1).then_inc(mask_step, 1)
            pool.wait_ge(mask_step, 4)
            nc.gpsimd.affine_select(out=bandf, in_=bandf, compare_op=ALU.is_ge, fill=0.0, base=TAIL,
                                    pattern=[[-1, GROUPS_T * WIN]], channel_multiplier=1)
            nc.gpsimd.affine_select(out=pick_f, in_=pick_f, compare_op=ALU.not_equal, fill=1.0, base=-LO,
                                    pattern=[[-1, E], [0, H]], channel_multiplier=1).then_inc(mask_step, 1)
            for e in range(E):
                nc.gpsimd.memset(rank[:, e:e + 1], float(E - e))
            nc.gpsimd.memset(half_neg[:, :], -0.5).then_inc(const_set, 1)
            pool.wait_ge(mask_step, 5)
            nc.gpsimd.tensor_copy(picker[:, :, :], pick_f).then_inc(prep_pool, 1)

            for k in range(KCH + 1):
                if k < KCH:
                    j = k // (WIN // RC)
                    pool.wait_ge(k_ev, j + 1)
                    pool.wait_ge(q_ev, j + 1)
                    if k >= 2:
                        pool.wait_ge(tl_dve, RP * (k - 1))
                        pool.wait_ge(tl_pool, k - 1)
                    add_window(nc.gpsimd, k, RP).then_inc(sum_pool, 1)
                if k >= 1:
                    pool.wait_ge(tanh_f, k)
                    pool.wait_ge(tanh_h, k)
                    at_least(pool, f_mm, k - 2)
                    low_part(nc.gpsimd, k - 1, RP).then_inc(tl_pool, 1)

            def split(hi, lo, src, after=None):
                nc.gpsimd.tensor_copy(hi, src).then_inc(prep_pool, 1)
                n[0] += 1
                pool.wait_ge(prep_pool, n[0])
                nc.gpsimd.tensor_tensor(lo, src, f32(hi), ALU.subtract)

            n = [1]
            pool.wait_ge(const_set, 1)
            for j in range(2):
                pool.wait_ge(ln1_var, j + 1)
                nc.gpsimd.tensor_tensor(ln[:, 5, :], ln[:, 4, :], half_neg[:, :], ALU.pow).then_inc(ln1_pow, 1)
                pool.wait_ge(ln1_pow, 2 * j + 1)
                nc.gpsimd.tensor_tensor(ln[:, 6, :], ln[:, 0, :], ln[:, 5, :], ALU.mult).then_inc(ln1_pow, 1)
                if j == 0:
                    pool.wait_ge(ffnw_in, FFNW)
                    split(gate_h[:, :], gate_l[:, :], gatew[:, :])
                    split(b2_h[:, :], b2_l[:, :], b2s[:, :])
                    split(w2_hl[:, :, 0, :], w2_hl[:, :, 1, :], w2s[:, :, :])
            for half in (slice(0, E // 2), slice(E // 2, E)):
                split(w1_h[:, half, :], w1_l[:, half, :], w1s[:, half, :])
            nc.gpsimd.memset(f32(cwS[:, :]), 0.0).then_inc(prep_pool, 1)
            pool.wait_ge(n1_done, B)
            for b in range(B):
                nc.gpsimd.tensor_tensor(h0[:, b, :, :], h0[:, b, :, :], b2b[:, :, :].to_broadcast([P, NT, C]),
                                        ALU.add).then_inc(h0_off, 1)
            pool.wait_ge(h0_off, B)

            links = [0]

            def link(ins):
                links[0] += 1
                ins.then_inc(pool_chain, 1)
                pool.wait_ge(pool_chain, links[0])

            def post(b, part):
                def wide(t):
                    return t[:, :, :].to_broadcast([P, NT, C])

                o = ob[:, b % 2, :, :]
                if part == 0:
                    pool.wait_ge(o_read, 2 * b + 2)
                    link(nc.gpsimd.tensor_tensor(o, o, ol[:, b % 2, :, :], ALU.add))
                    nc.gpsimd.tensor_tensor(o, o, wide(projb), ALU.add).then_inc(o_bias, 1)
                if part == 1:
                    pool.wait_ge(var2, b + 1)
                    link(nc.gpsimd.tensor_tensor(ln2[:, 5, :], ln2[:, 4, :], half_neg[:, 0:NT], ALU.pow))
                    nc.gpsimd.tensor_tensor(ln2[:, 6, :], ln2[:, 0, :], ln2[:, 5, :], ALU.mult).then_inc(s2_pow, 1)
                if part == 2:
                    pool.wait_ge(s2_done, b + 1)
                    link(nc.gpsimd.tensor_tensor(o, o, wide(g2b), ALU.mult))
                    nc.gpsimd.tensor_tensor(h1[:, b, :, :], o, h0[:, b, :, :], ALU.add).then_inc(h1_done, 1)
                if part == 3:
                    pool.wait_ge(var3, b + 1)
                    link(nc.gpsimd.tensor_tensor(ln3[:, 5, :], ln3[:, 4, :], half_neg[:, 0:NT], ALU.pow))
                    nc.gpsimd.tensor_tensor(ln3[:, 6, :], ln3[:, 0, :], ln3[:, 5, :], ALU.mult).then_inc(s3_pow, 1)

            for b in range(B - 1):
                for part in range(4):
                    post(b, part)

            for k in range(KC):
                for b, part in POOL_POST.get(S0 + k, ()):
                    post(b, part)
                if k < KC and k % E not in HI_DVE:
                    pool.wait_ge(gh_act, k + 1 - n_dve(k + 1))
                    at_least(pool, down_mm, k - RH + 1)
                    nc.gpsimd.tensor_tensor(gl[:, k % RH, :], gw[:, k % RG, :], f32(gh[:, k % RH, :]),
                                            ALU.subtract).then_inc(gl_pool, 1)

        @block.vector
        def _(dve):
            nc.vector.memset(xT[:, :, L:NP], 0.0).then_inc(pad_set, 1)
            nc.vector.memset(xr[EDGE:128, :, NT - 1, :, :], 0.0).then_inc(pad_set, 1)
            nc.vector.memset(b2s[:, :], 0.0).then_inc(b2_blank, 1)
            nc.vector.memset(f32(v9[:, :, :, :, :]), 0.0)
            for j in range(2):
                nc.vector.memset(qbuf[:, j, 0:4], 0.0)
                nc.vector.memset(qbuf[:, j, 4 + NP:QKW], 0.0)
                if j == 1:
                    nc.vector.memset(kbuf[:, j, NP:QKW], 0.0)
            nc.vector.memset(awE[:, :, 0:EDGE], 0.0)
            nc.vector.memset(kbuf[:, 0, NP:QKW], 0.0).then_inc(edge_set, 1)
            dve.wait_ge(edge_set, 1)
            dve.wait_ge(tokw_in, TOKW)
            nine = [128, WIN, 2]
            v_high, v_low = (bass.AP(v9, 2 * n, [[4 * WIN * WIN, 128], [4 * WIN + 4, WIN], [1, 2]]) for n in range(2))
            nc.vector.tensor_copy(v_high, v2[:, :].unsqueeze(1).to_broadcast(nine)).then_inc(prep_dve, 1)
            dve.wait_ge(prep_dve, 1)
            nc.vector.tensor_tensor(v_low, v2[:, :].unsqueeze(1).to_broadcast(nine), f32(v_high),
                                    ALU.subtract).then_inc(prep_dve, 1)

            def queries(j):
                dve.wait_ge(qk_mm, j + 1)
                nc.vector.tensor_scalar(cols(qbuf[:, j, 4:4 + NP]), halves(6), tokb[:, 0:1], None,
                                        ALU.add).then_inc(q_ev, 1)

            def weights():
                dve.wait_ge(attw_in, ATTW)
                w = wqkv[:, 0:2 * C].rearrange("p (n c) -> p n c", n=2).unsqueeze(2).to_broadcast([128, 2, 2, C])
                nc.vector.tensor_scalar(wqk[:, :, :, :], w, gcol[:, 0:1], None, ALU.mult).then_inc(prep_dve, 1)
                dve.wait_ge(prep_dve, 3)
                flat_w = wqk[:, :, :, :].rearrange("p n d c -> p n (d c)")
                nc.vector.tensor_copy(wqk_h[:, :, :], flat_w).then_inc(prep_dve, 1)
                dve.wait_ge(prep_dve, 4)
                nc.vector.tensor_tensor(wqk_l[:, :, :], flat_w, f32(wqk_h[:, :, :]),
                                        ALU.subtract).then_inc(prep_dve, 1)

            def weights_out():
                dve.wait_ge(prep_mm, 3)
                dve.wait_ge(prep_act, 1)
                nc.vector.tensor_tensor(qkc[:, :], ps[:, 2, 0:2], qkb[:, :], ALU.add).then_inc(prep_dve, 1)
                nc.vector.tensor_tensor(tvc[:, :], ps[0:C, 2, 2:3], bvc[:, :], ALU.add).then_inc(prep_dve, 1)

            def values_folded():
                dve.wait_ge(prep_mm, 4)
                dve.wait_ge(ffnw_in, FFNW)
                nc.vector.tensor_scalar(wvp[:, :], ps[:, 2, 128:128 + C], gcol[:, 0:1], scalec[:, 0:1], ALU.mult,
                                        ALU.mult).then_inc(prep_dve, 1)
                dve.wait_ge(prep_dve, 8)
                nc.vector.tensor_copy(wvp_h[:, :], wvp[:, :]).then_inc(prep_dve, 1)
                dve.wait_ge(prep_dve, 9)
                nc.vector.tensor_tensor(wvp_l[:, :], wvp[:, :], f32(wvp_h[:, :]), ALU.subtract).then_inc(prep_dve, 1)
                nc.vector.scalar_tensor_tensor(out=projb[:, 0, :], in0=ps[0:P, 2, 256:256 + C],
                                               scalar=scalec[0:P, 0:1], in1=projb[:, 0, :], op0=ALU.mult,
                                               op1=ALU.add).then_inc(prep_dve, 1)

            def window_softmax(j):
                f = ps[0:P, 4 + j, 0:NT * WIN * 4].rearrange("p (i r l h) -> p i r l h", r=WIN, l=2, h=2)
                e = es[:, j, :, :].rearrange("p (h i) r -> p h i r", h=2)
                dve.wait_ge(fT_mm, j + 1)
                for h in range(2):
                    ins = nc.vector.tensor_reduce(e[:, h, :, :], f[:, :, :, :, h], AX.X, ALU.add)
                ins.then_inc(smax_chain, 1)
                dve.wait_ge(smax_chain, 4 * j + 1)
                nc.vector.tensor_reduce(mx[:, j, :], es[:, j, :, :], AX.X, ALU.max).then_inc(smax_chain, 1)
                dve.wait_ge(smax_chain, 4 * j + 2)
                nc.vector.tensor_tensor(es[:, j, :, :], es[:, j, :, :],
                                        mx[:, j, :].unsqueeze(2).to_broadcast([P, 2 * NT, WIN]),
                                        ALU.subtract).then_inc(shifted, 1)

            def window_weights(j):
                dve.wait_ge(wexp, j + 1)
                if j == 0:
                    dve.wait_ge(const_set, 1)
                else:
                    dve.wait_ge(awT_mm, 2)
                for h in range(2):
                    ins = nc.vector.tensor_tensor(
                        aw[:, NT * h:NT * h + NT, :].rearrange("p t (g r) -> p t g r", r=WIN),
                        es[:, j, NT * h:NT * h + NT, :].unsqueeze(2).to_broadcast([P, NT, GROUPS_T, WIN]),
                        band[:, :, :].unsqueeze(1).to_broadcast([P, NT, GROUPS_T, WIN]), ALU.mult)
                    ins.then_inc(aw_done, 1)
                nc.vector.tensor_reduce(mx[:, j, :], es[:, j, :, :], AX.X, ALU.add).then_inc(smax_chain, 1)
                dve.wait_ge(smax_chain, 4 * j + 3)
                nc.vector.reciprocal(rs[:, j, :], mx[:, j, :]).then_inc(smax_chain, 1)
                dve.wait_ge(smax_chain, 4 * j + 4)

            queries(0)
            for k in range(KCH + 1):
                if k < KCH:
                    j = k // (WIN // RC)
                    dve.wait_ge(k_ev, j + 1)
                    dve.wait_ge(q_ev, j + 1)
                    if k >= 2:
                        dve.wait_ge(tl_dve, RP * (k - 1))
                        dve.wait_ge(tl_pool, k - 1)
                    for r in range(RP):
                        add_window(nc.vector, k, r).then_inc(sum_dve, 1)
                if k == 0:
                    queries(1)
                    nc.vector.memset(pr[:, :, NW:NP], 0.0).then_inc(edge_set, 1)
                    weights()
                if k >= 1:
                    dve.wait_ge(tanh_f, k)
                    dve.wait_ge(tanh_h, k)
                    at_least(dve, f_mm, k - 2)
                    for r in range(RP):
                        low_part(nc.vector, k - 1, r).then_inc(tl_dve, 1)
                if k == 1:
                    weights_out()
                if k == 2:
                    values_folded()
                if k == KCH // 2 + 1:
                    window_softmax(0)
                if k == KCH // 2 + 2:
                    window_weights(0)
            window_softmax(1)

            def row_moments(chain, src, stats, w, var_scale, eps):
                for i in range(stats.shape[1]):
                    ins = nc.vector.bn_stats(stats[:, i, :], src[:, i, :])
                chain(ins)
                nc.vector.tensor_tensor(w[:, 7, :], stats[:, :, 1], stats[:, :, 4], ALU.add)
                nc.vector.tensor_tensor(w[:, 2, :], stats[:, :, 2], stats[:, :, 5], ALU.add)
                chain(nc.vector.tensor_tensor(w[:, 1, :], stats[:, :, 1], stats[:, :, 4], ALU.subtract))
                chain(nc.vector.tensor_tensor(w[:, 3, :], w[:, 1, :], w[:, 1, :], ALU.mult))
                chain(nc.vector.scalar_tensor_tensor(out=w[:, 3, :], in0=w[:, 3, :], scalar=C / 4.0, in1=w[:, 2, :],
                                                     op0=ALU.mult, op1=ALU.add))
                chain(nc.vector.tensor_scalar(w[:, 0, :], w[:, 7, :], -0.5, None, ALU.mult))
                return nc.vector.tensor_scalar(w[:, 4, :], w[:, 3, :], var_scale, eps, ALU.mult, ALU.add)

            lc = [0]

            def ln1_link(ins):
                lc[0] += 1
                ins.then_inc(ln1_chain, 1)
                dve.wait_ge(ln1_chain, lc[0])

            def first_norm(j):
                for hf in range(2):
                    b = 2 * j + hf
                    dve.wait_ge(tok_mm, b + 1)
                    o = ps[0:P, hf, 0:NT * C].rearrange("p (i c) -> p i c", c=C)
                    r = rs[:, j, NT * hf:NT * hf + NT].unsqueeze(2).to_broadcast([P, NT, C])
                    nc.vector.tensor_tensor(h0[:, b, :, :], o, r, ALU.mult).then_inc(h0_out, 1)
                dve.wait_ge(h0_out, 2 * j + 2)
                if j == 1:
                    dve.wait_ge(n1_done, 2)
                rows = h0[:, 2 * j:2 * j + 2, :, :].rearrange("p b i c -> p (b i) c")
                row_moments(ln1_link, rows, st, ln, (1.0 + EPS) / C, EPS * EPS).then_inc(ln1_var, 1)

            def row_split(b):
                t = 4 + 2 * (b % 2)
                dve.wait_ge(hS_h, b + 1)
                nc.vector.tensor_tensor(cols(hS[C:128, b, :]), ps[C:128, t:t + 2, 0:HALF], cols(f32(hS[C:128, b, :])),
                                        ALU.subtract).then_inc(hS_l, 1)

            def first_splits(b):
                dve.wait_ge(kS_h, b + 1)
                nc.vector.scalar_tensor_tensor(out=cols(kS[C:128, b, :]), in0=ps[C:128, 2:4, 0:HALF],
                                               scalar=qkc[C:128, 1:2], in1=cols(f32(kS[C:128, b, :])),
                                               op0=ALU.add, op1=ALU.subtract).then_inc(kS_l, 1)
                dve.wait_ge(q_h, b + 1)
                nc.vector.scalar_tensor_tensor(out=cols(qL[b]), in0=halves(0), scalar=qkc[:, 0:1],
                                               in1=cols(f32(qH[:, b, :])), op0=ALU.add,
                                               op1=ALU.subtract).then_inc(q_l, 1)
                dve.wait_ge(v_h, b + 1)
                v = ps[0:P, 4 + 2 * (b % 2), 0:NT * C].rearrange("p (i c) -> p i c", c=C)
                nc.vector.tensor_tensor(v_hl[:, b, :, 1, :], v, f32(v_hl[:, b, :, 0, :]), ALU.subtract).then_inc(v_l, 1)

            window_weights(1)
            first_norm(0)
            first_norm(1)
            for b in range(B + 1):
                if b < B:
                    row_split(b)
                if b >= 1:
                    first_splits(b - 1)

            dve.wait_ge(hankel_in, 16)
            dve.wait_ge(prep_dve, 11)

            def scores(n):
                i = n % NT
                dve.wait_ge(s_mm, n + 1)
                at_least(dve, p_done, n - 1)
                bias = bass.AP(hankel, P * i + NW - 1, [[ZW, P], [-MH, 2], [-1, MH]])
                s = bass.AP(ps, 2 * (i % 2) * 512, [[8 * 512, P], [513, 2], [1, MH]])
                nc.vector.tensor_tensor_reduce(
                    out=sc[:, i % 2, :].rearrange("p (h m) -> p h m", h=2), in0=s, in1=bias, scale=-1.0, scalar=BIG,
                    op0=ALU.add, op1=ALU.min, accum_out=nmax[:, i % 2:i % 2 + 1]).then_inc(s_max, 1)

            def probs_low(n):
                i = n
                dve.wait_ge(pT_hi, n + 1)
                at_least(dve, pv_mm, n - 1)
                nc.vector.tensor_tensor(cols(pT_l[:, i % 2, :]), halves(4, P), cols(f32(pT_h[:, i % 2, :])),
                                        ALU.subtract).then_inc(pT_lo, 1)

            def attention_out(n):
                b, g = n // 2, n % 2
                tiles = slice(3 * g, 3 * g + 3)
                dve.wait_ge(p_done, 3 * n + 3)
                nc.vector.reciprocal(rinv[:, tiles], rsum[:, tiles]).then_inc(rinv_done, 1)
                dve.wait_ge(rinv_done, n + 1)
                dve.wait_ge(pv_mm, 3 * n + 3)
                at_least(dve, h1_done, b - 1)
                o = ps[0:P, 6, 0:3 * 2 * C].rearrange("p (i l c) -> p i l c", l=2, c=C)
                r = rinv[:, tiles].unsqueeze(2).to_broadcast([P, 3, C])
                nc.vector.tensor_tensor(ob[:, b % 2, tiles, :], o[:, :, 0, :], r, ALU.mult)
                nc.vector.tensor_tensor(ol[:, b % 2, tiles, :], o[:, :, 1, :], r, ALU.mult).then_inc(o_read, 1)

            links = [0]

            def post(b, part):
                def link(ins):
                    links[0] += 1
                    ins.then_inc(post_dve, 1)
                    dve.wait_ge(post_dve, links[0])

                def low_rows(h):
                    dve.wait_ge(nS_h, 2 * b + h + 1)
                    c = slice(HALF * h, HALF * h + HALF)
                    nc.vector.tensor_tensor(nS[C:128, b, c], ps[C:128, 7, 0:HALF], f32(nS[C:128, b, c]),
                                            ALU.subtract).then_inc(nS_l, 1)

                if part == 0:
                    dve.wait_ge(o_bias, b + 1)
                    row_moments(link, ob[:, b % 2, :, :], st2, ln2, 1.0 / C, EPS).then_inc(var2, 1)
                if part == 1:
                    dve.wait_ge(h1_done, b + 1)
                    row_moments(link, h1[:, b, :, :], st2, ln3, 1.0 / C, EPS).then_inc(var3, 1)
                if part == 2:
                    low_rows(0)
                if part == 3:
                    low_rows(1)
                def wide(t):
                    return t.unsqueeze(2).to_broadcast([P, NT, E])

                lg, eq, p, s1, s2 = (pt[:, n, :, :] for n in range(5))
                top = pm[:, 0, :]
                rk = rank[:, :].unsqueeze(1).to_broadcast([P, NT, E])

                def pick(src, sel):
                    link(nc.vector.tensor_reduce(top, src, AX.X, ALU.max))
                    link(nc.vector.tensor_tensor(eq, src, wide(top), ALU.is_equal))
                    link(nc.vector.tensor_tensor(eq, eq, rk, ALU.mult))
                    link(nc.vector.tensor_reduce(pm[:, 3, :], eq, AX.X, ALU.max))
                    link(nc.vector.tensor_tensor(sel, eq, wide(pm[:, 3, :]), ALU.is_equal))

                if part == 4:
                    dve.wait_ge(post_mm, 6 * b + 3)
                    link(nc.vector.tensor_tensor(lg, ps[0:P, 7, 0:NT * E].rearrange("p (i e) -> p i e", e=E),
                                                 gateb[:, :, :].to_broadcast([P, NT, E]), ALU.add))
                    link(nc.vector.tensor_reduce(top, lg, AX.X, ALU.max))
                    nc.vector.tensor_tensor(lg, lg, wide(top), ALU.subtract).then_inc(lg_shift, 1)
                if part == 5:
                    dve.wait_ge(lg_exp, b + 1)
                    link(nc.vector.tensor_reduce(pm[:, 1, :], lg, AX.X, ALU.add))
                    link(nc.vector.reciprocal(pm[:, 2, :], pm[:, 1, :]))
                    link(nc.vector.tensor_tensor(p, lg, wide(pm[:, 2, :]), ALU.mult))
                    pick(p, s1)
                if part == 6:
                    link(nc.vector.scalar_tensor_tensor(out=lg, in0=s1, scalar=-2.0, in1=p, op0=ALU.mult, op1=ALU.add))
                    pick(lg, s2)
                    link(nc.vector.tensor_tensor(s1, s1, s2, ALU.add))
                    nc.vector.tensor_tensor(cws[:, :, :], s1, p, ALU.mult).then_inc(cw_done, 1)
                if part in (7, 8):
                    h = part - 7
                    dve.wait_ge(cw_h, 2 * b + h + 1)
                    c = slice(NP * b + HALF * h, NP * b + HALF * h + HALF)
                    nc.vector.tensor_tensor(cwS[LO:LO + E, c], ps[0:E, 7, 0:HALF], f32(cwS[0:E, c]),
                                            ALU.subtract).then_inc(cw_l, 1)
                if part == 9:
                    dve.wait_ge(post_mm, 6 * b + 6)
                    nc.vector.tensor_tensor(h1[:, b, :, :], ps[0:P, 7, 0:NT * C].rearrange("p (i c) -> p i c", c=C),
                                            h1[:, b, :, :], ALU.add).then_inc(base_done, 1)

            scores(0)
            scores(1)
            for n in range(B * NT):
                if n >= 3 and n % 3 == 0:
                    attention_out(n // 3 - 1)
                probs_low(n)
                if n + 2 < B * NT:
                    scores(n + 2)
                for b, part in DVE_POST.get(n, ()):
                    post(b, part)
            attention_out(2 * B - 1)

            def y_down(n):
                b, hf = n // 2, n % 2
                tiles = slice(3 * hf, 3 * hf + 3)
                dve.wait_ge(yT_mm, n + 1)
                y = ps[0:P, 6, 0:3 * 128].rearrange("p (t l c) -> p t l c", l=2, c=C)
                nc.vector.tensor_tensor(yo[:, b, tiles, :], y[:, :, 0, :], h1[:, b, tiles, :], ALU.add).then_inc(y_add, 1)
                dve.wait_ge(y_add, n + 1)
                nc.vector.tensor_tensor(yo[:, b, tiles, :], y[:, :, 1, :], yo[:, b, tiles, :], ALU.add).then_inc(y_sum, 1)

            for k in range(KC):
                e = k % E
                for b, part in DVE_POST.get(S0 + k, ()):
                    post(b, part)
                dve.wait_ge(gelu_done, k + 1)
                dve.wait_ge(cb_mm, k + 1)
                at_least(dve, gl_pool, k - RG + 1 - n_dve(k - RG + 1) if k >= RG else 0)
                nc.vector.tensor_tensor(gw[:, k % RG, :], ge[:, k % RG, :], ps[:, 2 + k % 2, 0:HALF],
                                        ALU.mult).then_inc(gw_done, 1)
                if e in HI_DVE:
                    at_least(dve, down_mm, k - RH + 1)
                    dve.wait_ge(gw_done, k + 1)
                    nc.vector.tensor_copy(gh[:, k % RH, :], gw[:, k % RG, :]).then_inc(gh_dve, 1)
                    dve.wait_ge(gh_dve, n_dve(k + 1))
                    nc.vector.tensor_tensor(gl[:, k % RH, :], gw[:, k % RG, :], f32(gh[:, k % RH, :]),
                                            ALU.subtract).then_inc(gl_dve, 1)
                if e == E - 1 and k > E:
                    y_down(k // E - 1)
            y_down(KC // E - 1)

        def y_up(act, n):
            act.wait_ge(down_mm, E * (n + 1))
            at_least(act, yT_mm, n - 1)
            nc.scalar.activation(ysb[:, n % 2, :], ps[:, 4 + n % 2, 0:HALF], ACT.Copy).then_inc(y_copied, 1)

        @block.scalar
        def _(act):
            def keys(j):
                act.wait_ge(qk_mm, j + 1)
                if j == 0:
                    act.wait_ge(edge_set, 1)
                nc.scalar.activation(cols(kbuf[:, j, 0:NP]), halves(4), ACT.Copy).then_inc(k_ev, 1)

            def tanhs(k):
                act.wait_ge(sum_dve, RP * (k + 1))
                act.wait_ge(sum_pool, k + 1)
                at_least(act, f_mm, k - 1)
                nc.scalar.activation(th[:, k % 2, :, 0:TW], ts[:, k % 2, :, :], ACT.Tanh).then_inc(tanh_h, 1)
                nc.scalar.activation(ts[:, k % 2, :, :], ts[:, k % 2, :, :], ACT.Tanh).then_inc(tanh_f, 1)

            def window_exp(j):
                act.wait_ge(shifted, j + 1)
                nc.scalar.activation(es[:, j, :, :], es[:, j, :, :], ACT.Exp).then_inc(wexp, 1)

            def scores_out(j):
                act.wait_ge(f_mm, (j + 1) * (WIN // RC))
                at_least(act, fT_mm, j)
                nc.scalar.activation(cols(frow[:, :]), halves(2 * j, 4 * WIN), ACT.Copy).then_inc(f_copied, 1)

            keys(0)
            for k in range(KCH):
                tanhs(k)
                if k == 0:
                    keys(1)
                    act.wait_ge(prep_mm, 3)
                    nc.scalar.activation(wvt[:, :], ps[0:C, 2, 64:64 + C], ACT.Copy).then_inc(prep_act, 1)
                if k == KCH // 2:
                    scores_out(0)
                if k == KCH // 2 + 1:
                    window_exp(0)

            def weights_up(b):
                act.wait_ge(awT_mm, b + 1)
                at_least(act, tok_mm, b)
                nc.scalar.activation(awT[:, :, :].rearrange("p (h i) n -> p h (i n)", h=2), halves(6, P), ACT.Copy)
                nc.scalar.activation(awE[:, 0:4, EDGE:P], ps[0:TAIL, 6, HALF:HALF + 4 * NE]
                                     .rearrange("p (i n) -> p i n", n=NE), ACT.Copy)
                nc.scalar.activation(awE[:, 4, EDGE:P], ps[0:TAIL, 7, HALF:HALF + NE], ACT.Copy).then_inc(awT_ev, 1)

            def normalize(b):
                j, hf = b // 2, b % 2
                act.wait_ge(ln1_pow, 2 * j + 2)
                at_least(act, hT_mm, b - 1)
                for i in range(NT):
                    n = NT * hf + i
                    ins = nc.scalar.activation(n1[:, hf, i, :, :], h0[:, b, i, :].unsqueeze(1).to_broadcast([P, 2, C]),
                                               ACT.Identity, bias=ln[:, 6, n:n + 1], scale=ln[:, 5, n:n + 1])
                ins.then_inc(n1_done, 1)

            def row_high(b):
                act.wait_ge(hT_mm, b + 1)
                nc.scalar.activation(cols(hS[:, b, :]), halves(4 + 2 * (b % 2)), ACT.Copy).then_inc(hS_h, 1)

            def high_parts(b):
                act.wait_ge(k_mm, b + 1)
                nc.scalar.activation(cols(kS[:, b, :]), halves(2), ACT.Identity, bias=qkc[:, 1:2]).then_inc(kS_h, 1)
                act.wait_ge(q_mm, b + 1)
                nc.scalar.activation(cols(qH[:, b, :]), halves(0), ACT.Identity, bias=qkc[:, 0:1]).then_inc(q_h, 1)
                act.wait_ge(v_mm, b + 1)
                nc.scalar.activation(v_hl[:, b, :, 0, :], ps[0:P, 4 + 2 * (b % 2), 0:NT * C]
                                     .rearrange("p (i c) -> p i c", c=C), ACT.Copy).then_inc(v_h, 1)

            weights_up(0)
            scores_out(1)
            window_exp(1)
            for b in range(1, B):
                weights_up(b)
            act.wait_ge(prep_dve, 11)
            normalize(0)
            normalize(1)
            row_high(0)
            for b in range(1, B + 1):
                if b < B:
                    row_high(b)
                if b + 1 < B:
                    normalize(b + 1)
                high_parts(b - 1)

            def probs(n):
                b, i = n // NT, n % NT
                act.wait_ge(s_max, n + 1)
                at_least(act, pT_mm, n - 1)
                if i % 3 == 0:
                    at_least(act, rinv_done, 2 * (b - 1) + i // 3 + 1)
                nc.scalar.activation(pr[:, i % 2, 0:NW], sc[:, i % 2, :], ACT.Exp, bias=nmax[:, i % 2:i % 2 + 1],
                                     scale=-1.0, accum_out=rsum[:, i:i + 1]).then_inc(p_done, 1)

            def probs_high(n):
                i = n
                act.wait_ge(pT_mm, n + 1)
                at_least(act, pv_mm, n - 1)
                nc.scalar.activation(cols(pT_h[:, i % 2, :]), halves(4, P), ACT.Copy).then_inc(pT_hi, 1)

            def post(b, part):
                if part == 0:
                    act.wait_ge(s2_pow, b + 1)
                    for i in range(NT):
                        o = ob[:, b % 2, i, :]
                        ins = nc.scalar.activation(o, o, ACT.Identity, bias=ln2[:, 6, i:i + 1], scale=ln2[:, 5, i:i + 1])
                    ins.then_inc(s2_done, 1)
                if part == 1:
                    act.wait_ge(s3_pow, b + 1)
                    at_least(act, post_mm, 6 * (b - 1) + 2)
                    for i in range(NT):
                        ins = nc.scalar.activation(n3[:, i, :, :], h1[:, b, i, :].unsqueeze(1).to_broadcast([P, 2, C]),
                                                   ACT.Identity, bias=ln3[:, 6, i:i + 1], scale=ln3[:, 5, i:i + 1])
                    ins.then_inc(n3_done, 1)
                if part in (2, 3):
                    h = part - 2
                    act.wait_ge(post_mm, 6 * b + h + 1)
                    nc.scalar.activation(nS[:, b, HALF * h:HALF * h + HALF], ps[:, 7, 0:HALF],
                                         ACT.Copy).then_inc(nS_h, 1)
                if part == 4:
                    act.wait_ge(lg_shift, b + 1)
                    nc.scalar.activation(pt[:, 0, :, :], pt[:, 0, :, :], ACT.Exp).then_inc(lg_exp, 1)
                if part > 4:
                    h = part - 5
                    act.wait_ge(post_mm, 6 * b + h + 4)
                    if b == 0 and h == 0:
                        act.wait_ge(prep_pool, 7)
                    nc.scalar.activation(cwS[0:E, NP * b + HALF * h:NP * b + HALF * h + HALF], ps[0:E, 7, 0:HALF],
                                         ACT.Copy).then_inc(cw_h, 1)

            probs(0)
            for n in range(B * NT):
                probs_high(n)
                if n + 1 < B * NT:
                    probs(n + 1)
                for b, part in ACT_POST.get(n, ()):
                    post(b, part)

            for k in range(KC + 1):
                for b, part in ACT_POST.get(S0 + k, ()):
                    post(b, part)
                if k < KC:
                    act.wait_ge(up_mm, k + 1)
                    at_least(act, gw_done, k - RG + 1)
                    nc.scalar.activation(ge[:, k % RG, :], ps[:, k % 2, 0:HALF], ACT.Gelu,
                                         bias=b1s[:, k % E:k % E + 1]).then_inc(gelu_done, 1)
                m = k - 1
                if m >= 0 and m % E not in HI_DVE:
                    act.wait_ge(gw_done, m + 1)
                    at_least(act, down_mm, m - RH + 1)
                    nc.scalar.activation(gh[:, m % RH, :], gw[:, m % RG, :], ACT.Copy).then_inc(gh_act, 1)
                if m % E == 4 and m > E:
                    y_up(act, m // E - 1)
            y_up(act, KC // E - 1)

        @block.tensor
        def _(pe):
            mm, tp = nc.tensor.matmul, nc.tensor.transpose

            def split_mm(o, pairs, start=True, stop=True):
                for n, (a, b) in enumerate(pairs):
                    ins = mm(o, a, b, start=start and n == 0, stop=stop and n == len(pairs) - 1)
                return ins

            def keys_queries(j):
                pe.wait_ge(x_in[j], 16)
                if j == 1:
                    pe.wait_ge(k_ev, 1)
                    pe.wait_ge(q_ev, 1)
                for w, bank in ((wk2, 4), (wq2, 6)):
                    for h in range(2):
                        ins = mm(ps[:, bank + h, 0:HALF], w[:, :], xT[:, j, HALF * h:HALF * h + HALF],
                                 start=True, stop=True)
                ins.then_inc(qk_mm, 1)

            def weights():
                pe.wait_ge(attw_in, ATTW)
                pe.wait_ge(ident_set, 1)
                w = wqkv[0:C, 0:2 * C].rearrange("p (n c) -> p n c", n=2)
                for n in range(2):
                    for half in (slice(0, C), slice(C, 128)):
                        ins = mm(ps[half, 2, n:n + 1], w[:, n, :], bcol[0:C, :], start=True, stop=True)
                    ins.then_inc(prep_mm, 1)
                mm(ps[0:C, 2, 2:3], wqkv[0:C, 2 * C:3 * C], bcol[0:C, :], start=True, stop=True)
                tp(ps[0:C, 2, 64:64 + C], wqkv[0:C, 2 * C:3 * C], ident[0:C, 0:C]).then_inc(prep_mm, 1)

            def value_weights():
                pe.wait_ge(prep_act, 1)
                pe.wait_ge(prep_dve, 7)
                for half in (slice(0, C), slice(C, 128)):
                    ins = mm(ps[half, 2, 128:128 + C], wvt[:, :], wproj[:, :], start=True, stop=True)
                mm(ps[0:P, 2, 256:256 + C], tvc[:, 0:1].to_broadcast([C, P]), wproj[:, :],
                   start=True, stop=True).then_inc(prep_mm, 1)

            def window_scores(k):
                j, q = k // (WIN // RC), k % (WIN // RC)
                if k == 0:
                    pe.wait_ge(prep_dve, 2)
                if k == WIN // RC:
                    pe.wait_ge(prep_dve, 11)
                for part, x in enumerate((th, tl)):
                    if part == 0:
                        pe.wait_ge(tanh_h, k + 1)
                    else:
                        pe.wait_ge(tl_dve, RP * (k + 1))
                        pe.wait_ge(tl_pool, k + 1)
                    for r in range(RC):
                        res = RC * q + r
                        w = v9[:, res, :, :, :].rearrange("p r l h -> p (r l h)")
                        for h in range(2):
                            c0 = HALF * h + TAIL - res
                            ins = mm(ps[0:4 * WIN, 2 * j + h, 0:HALF], w, x[:, k % 2, r, c0:c0 + HALF],
                                     start=(part == 0 and res == 0), stop=(part == 1 and res == WIN - 1))
                ins.then_inc(f_mm, 1)

            def window_rows(j):
                pe.wait_ge(f_copied, j + 1)
                for i in range(NT):
                    m = 4 * WIN * i
                    ins = tp(ps[0:P, 4 + j, m:m + 4 * WIN], frow[:, P * i:P * i + P], ident[0:4 * WIN, 0:4 * WIN])
                ins.then_inc(fT_mm, 1)

            def window_up(b):
                j, hf = b // 2, b % 2
                pe.wait_ge(aw_done, b + 1)
                at_least(pe, awT_ev, b)
                for i in range(NT):
                    tp(ps[0:P, 6 + i // 3, P * (i % 3):P * (i % 3) + P], aw[:, NT * hf + i, 0:P], ident[0:P, 0:P])
                for i in range(NT - 1):
                    o = ps[0:TAIL, 6 + i // 4, HALF + NE * (i % 4):HALF + NE * (i % 4) + NE]
                    ins = tp(o, aw[EDGE:P, NT * hf + i, P:P + TAIL], ident[EDGE:P, EDGE:P])
                ins.then_inc(awT_mm, 1)

            def window_out(b):
                j, hf = b // 2, b % 2
                pe.wait_ge(awT_ev, b + 1)
                if b == 0:
                    pe.wait_ge(xrow_in, 2 * B * 16)
                if b == 0:
                    pe.wait_ge(f_copied, 1)
                if b >= 2:
                    pe.wait_ge(h0_out, b - 1)
                for i in range(NT):
                    last = i == NT - 1
                    ins = mm(ps[0:P, b % 2, C * i:C * i + C], awT[:, i, :], xr[0:P, j, i, hf, :], start=True,
                             stop=last)
                    if not last:
                        ins = mm(ps[0:P, b % 2, C * i:C * i + C], awE[:, i, :], xr[0:TAIL, j, i + 1, hf, :],
                                 start=False, stop=True)
                ins.then_inc(tok_mm, 1)

            def rows_up(b):
                pe.wait_ge(n1_done, b + 1)
                at_least(pe, v_l, b - 1)
                if b == 0:
                    pe.wait_ge(shifted, 2)
                for i in range(NT):
                    ins = tp(ps[:, 4 + 2 * (b % 2) + i // 3, P * (i % 3):P * (i % 3) + P],
                             n1[:, b % 2, i, :, :].rearrange("p d c -> p (d c)"), ident[0:P, 0:P])
                ins.then_inc(hT_mm, 1)

            def project(b):
                pe.wait_ge(hS_h, b + 1)
                pe.wait_ge(hS_l, b + 1)
                at_least(pe, kS_l, b)
                for n, bank, done in ((1, 2, k_mm), (0, 0, q_mm)):
                    if n == 0:
                        at_least(pe, q_l, b)
                        if b == 0:
                            pe.wait_ge(h0_out, B)
                    for h in range(2):
                        x = hS[:, b, HALF * h:HALF * h + HALF]
                        ins = split_mm(ps[:, bank + h, 0:HALF], [(wqk_h[:, n, :], x), (wqk_l[:, n, :], x)])
                    ins.then_inc(done, 1)
                for i in range(NT):
                    x = hS[:, b, P * i:P * i + P]
                    ins = split_mm(ps[0:P, 4 + 2 * (b % 2), C * i:C * i + C], [(x, wvp_h[:, :]), (x, wvp_l[:, :])])
                ins.then_inc(v_mm, 1)

            pe.wait_ge(tokw_in, TOKW)
            keys_queries(0)
            keys_queries(1)
            weights()
            for k in range(KCH):
                window_scores(k)
                if k == 1:
                    value_weights()
                if k == KCH // 2:
                    window_rows(0)
                if k == KCH // 2 + 1:
                    window_up(0)
            window_rows(1)
            window_out(0)
            for b in range(1, B):
                window_up(b)
                window_out(b)
            rows_up(0)
            for b in range(1, B + 1):
                if b < B:
                    rows_up(b)
                project(b - 1)
            pe.wait_ge(kS_l, B)
            pe.wait_ge(q_l, B)
            pe.wait_ge(v_l, B)

            def scores(n):
                b, i = n // NT, n % NT
                at_least(pe, s_max, n - 1)
                for h in range(2):
                    keys = kS[:, b, (MH - 1) * h:(MH - 1) * h + MH + 1]
                    ins = split_mm(ps[0:P, 2 * (i % 2) + h, 0:MH + 1],
                                   [(qH[:, b, P * i:P * i + P], keys), (qL[b][:, P * i:P * i + P], keys)])
                ins.then_inc(s_mm, 1)

            def probs_up(n):
                i = n
                pe.wait_ge(p_done, n + 1)
                if n == 0:
                    pe.wait_ge(edge_set, 2)
                at_least(pe, pT_lo, n)
                for m in range(NT):
                    ins = tp(ps[0:P, 4 + m // 3, P * (m % 3):P * (m % 3) + P], pr[:, i % 2, P * m:P * m + P],
                             ident[0:P, 0:P])
                ins.then_inc(pT_mm, 1)

            def values(n):
                b, i = n // NT, n % NT
                if i % 3 == 0:
                    at_least(pe, o_read, n // 3)
                o = ps[0:P, 6, 2 * C * (i % 3):2 * C * (i % 3) + 2 * C]
                for part, (pT, ready) in enumerate(((pT_h, pT_hi), (pT_l, pT_lo))):
                    pe.wait_ge(ready, n + 1)
                    for m in range(NT):
                        ins = mm(o, pT[:, i % 2, P * m:P * m + P], v_hl[:, b, m, :, :].rearrange("p l c -> p (l c)"),
                                 start=(part == 0 and m == 0), stop=(part == 1 and m == NT - 1))
                ins.then_inc(pv_mm, 1)

            def post(b, step):
                if step < 2:
                    if step == 0:
                        pe.wait_ge(n3_done, b + 1)
                        at_least(pe, base_done, b)
                    else:
                        pe.wait_ge(nS_l, 2 * b + 1)
                    for i in range(3):
                        ins = tp(ps[:, 7, P * i:P * i + P],
                                 n3[:, 3 * step + i, :, :].rearrange("p d c -> p (d c)"), ident[0:P, 0:P])
                elif step == 2:
                    pe.wait_ge(nS_l, 2 * b + 2)
                    if b == 0:
                        pe.wait_ge(prep_pool, 7)
                    for i in range(NT):
                        x = nS[:, b, P * i:P * i + P]
                        ins = split_mm(ps[0:P, 7, E * i:E * i + E], [(x, gate_h[:, :]), (x, gate_l[:, :])])
                elif step < 5:
                    if step == 3:
                        pe.wait_ge(cw_done, b + 1)
                    else:
                        pe.wait_ge(cw_l, 2 * b + 1)
                    for i in range(3):
                        ins = tp(ps[0:E, 7, P * i:P * i + P], cws[:, 3 * (step - 3) + i, :], ident[0:P, 0:P])
                else:
                    pe.wait_ge(cw_l, 2 * b + 2)
                    for i in range(NT):
                        c = cwS[:, NP * b + P * i:NP * b + P * i + P]
                        ins = split_mm(ps[0:P, 7, C * i:C * i + C], [(c, b2_h[:, :]), (c, b2_l[:, :])])
                ins.then_inc(post_mm, 1)

            scores(0)
            scores(1)
            for n in range(B * NT):
                probs_up(n)
                if n + 2 < B * NT:
                    scores(n + 2)
                values(n)
                for b, step in PE_POST.get(n, ()):
                    post(b, step)

            def up(k):
                n, e = k // E, k % E
                b, hf = n // 2, n % 2
                x = nS[:, b, HALF * hf:HALF * hf + HALF]
                at_least(pe, gelu_done, k - 1)
                split_mm(ps[:, k % 2, 0:HALF], [(w1_h[:, e, :], x), (w1_l[:, e, :], x)]).then_inc(up_mm, 1)
                at_least(pe, gw_done, k - 1)
                mm(ps[:, 2 + k % 2, 0:HALF], picker[:, e, :], cwS[:, HALF * n:HALF * n + HALF],
                   start=True, stop=True).then_inc(cb_mm, 1)

            def down(k):
                n, e = k // E, k % E
                if e in HI_DVE:
                    pe.wait_ge(gl_dve, n_dve(k + 1))
                else:
                    pe.wait_ge(gl_pool, k + 1 - n_dve(k + 1))
                if e == 0:
                    at_least(pe, y_copied, n - 1)
                w = w2_hl[:, e, :, :].rearrange("p l c -> p (l c)")
                split_mm(ps[:, 4 + n % 2, 0:HALF], [(w, gh[:, k % RH, :]), (w, gl[:, k % RH, :])],
                         start=(e == 0), stop=(e == E - 1)).then_inc(down_mm, 1)

            def y_rows(n):
                pe.wait_ge(y_copied, n + 1)
                at_least(pe, y_sum, n)
                for t in range(3):
                    ins = tp(ps[0:P, 6, 128 * t:128 * t + 128], ysb[:, n % 2, P * t:P * t + P], ident[:, :])
                ins.then_inc(yT_mm, 1)

            pe.wait_ge(s_max, B * NT)
            LAG = 3
            for k in range(KC + LAG):
                for b, step in PE_POST.get(S0 + k, ()):
                    post(b, step)
                if k % (2 * E) == 0 and k < KC:
                    pe.wait_ge(base_done, k // (2 * E) + 1)
                if k == E:
                    pe.wait_ge(o_read, 2 * B)
                if k < KC:
                    up(k)
                if k >= LAG:
                    down(k - LAG)
                if k >= LAG and (k - LAG) % E == 3 and k - LAG > E:
                    y_rows((k - LAG) // E - 1)
            y_rows(KC // E - 1)


_INS = ['x', 'x_columns', 'L0_tok_W_qry', 'L0_tok_W_key', 'L0_tok_v', 'L0_tok_b', 'L0_attn_ln1_g', 'L0_attn_ln1_b',
        'L0_attn_qkv_w', 'L0_attn_qkv_b', 'L0_attn_bias_table', 'L0_attn_scale', 'L0_attn_proj_w',
        'L0_attn_proj_b', 'L0_attn_ln2_g', 'L0_attn_ln2_b', 'L0_ffn_gate_w', 'L0_ffn_gate_b', 'L0_ffn_W1',
        'L0_ffn_b1', 'L0_ffn_W2', 'L0_ffn_b2']


def kernel(**inputs):
    import numpy as _np
    import concourse.bacc as _bacc
    from concourse.bass_utils import run_bass_kernel_spmd as _run

    nc = _bacc.Bacc("TRN2", target_bir_lowering=False, num_devices=1)
    arrays, args = {}, []
    for name in _INS:
        a = _np.asarray(inputs['x' if name == 'x_columns' else name])
        if name == 'x_columns':
            a = a.transpose(0, 2, 1).reshape(B // 2, 2 * C, L)
        if name == 'L0_attn_bias_table':
            a = a[::-1]
        if name == 'L0_ffn_b1':
            a = a.T
        if name == 'L0_attn_scale':
            a = a.reshape(1, 1)
        a = _np.ascontiguousarray(a)
        arrays[f"in_{name}"] = a
        args.append(nc.dram_tensor(f"in_{name}", a.shape, mybir.dt.from_np(a.dtype), kind="ExternalInput").ap())
    args.append(nc.dram_tensor("out_0", (B, NW, C), F32, kind="ExternalOutput").ap())
    audio_tower(nc, *args)
    r = _run(nc, [arrays], core_ids=[0])
    return r.results[0]["out_0"]
```

```python
from contextlib import ExitStack

import concourse.bass as bass
from concourse import mybir

ALU = mybir.AluOpType
ACT = mybir.ActivationFunctionType
AX = mybir.AxisListType
F32 = mybir.dt.float32
F32R = mybir.dt.float32r

B, L, C = 4, 750, 64
WIN = 9
NW = L - WIN + 1
P = 14 * WIN
NT = -(-NW // P)
NP = NT * P
HALF = NP // 2
TAIL = WIN - 1
GROUPS = NP // WIN + 1
TW = GROUPS * WIN
QKW = 776
H, E = 128, 8
EPS = 1e-5
BIG = 3.0e38
TABLE = 1023
EDGE = 96
NE = P - EDGE
LO = 32
RC = 3
MH = NW // 2
LEAD = 2 * NW - 2 - (TABLE - 1)
ZW = (NT - 1) * P + NW
GROUPS_T = P // WIN + 1
EXT = ZW + P


def at_least(eng, sem, value):
    if isinstance(value, int) and value <= 0:
        return
    eng.wait_ge(sem, value)


def by_slot(*batches):
    slots = {}
    for b, parts in enumerate(batches):
        for part, slot in enumerate(parts):
            slots.setdefault(slot, []).append((b, part))
    return slots


def audio_tower(nc, xrow, xcol, w_qry, w_key, tok_v, tok_b, ln1_g, ln1_b, qkv_w, qkv_b, rtable, scale,
                proj_w, proj_b, ln2_g, ln2_b, gate_w, gate_b, w1, b1, w2, b2, out):
    with ExitStack() as ctx:
        def sb(name, shape, dt=F32):
            return ctx.enter_context(nc.sbuf_tensor(name, shape, dt))

        def sem(name):
            return ctx.enter_context(nc.semaphore(name))

        ps = ctx.enter_context(nc.psum_tensor("ps", [128, 8, 512], F32))
        table_ext = nc.dram_tensor("table_ext", (EXT,), F32)

        def f32(t):
            return t.bitcast(F32)

        ident = sb("ident", [128, 128])
        band = sb("band", [P, GROUPS_T, WIN])
        rank = sb("rank", [P, E])
        half_neg = sb("half_neg", [P, 2 * NT])
        wk2, wq2 = sb("wk2", [128, 128]), sb("wq2", [128, 128])
        v2 = sb("v2", [128, 2])
        v9 = sb("v9", [128, WIN, WIN, 2, 2], F32R)
        v9f = sb("v9f", [128, WIN, WIN, 2, 2])
        tokb = sb("tokb", [128, 1])
        gcol, bcol = sb("gcol", [128, 1]), sb("bcol", [128, 1])
        qkb = sb("qkb", [128, 2])
        qkc = sb("qkc", [128, 2])
        wqkv = sb("wqkv", [128, 3 * C])
        wqk = sb("wqk", [128, 2, 2, C])
        wqk_h, wqk_l = sb("wqk_h", [128, 2, 2 * C], F32R), sb("wqk_l", [128, 2, 2 * C], F32R)
        bvc, tvc = sb("bvc", [C, 1]), sb("tvc", [C, 1])
        wvt = sb("wvt", [C, C])
        wproj = sb("wproj", [C, C])
        wvp = sb("wvp", [128, C])
        wvp_h, wvp_l = sb("wvp_h", [128, C], F32R), sb("wvp_l", [128, C], F32R)
        scalec = sb("scalec", [128, 1])
        projb = sb("projb", [P, 1, C])
        g2b, b2b = sb("g2b", [P, 1, C]), sb("b2b", [P, 1, C])
        gatew = sb("gatew", [128, E])
        gate_h, gate_l = sb("gate_h", [128, E], F32R), sb("gate_l", [128, E], F32R)
        gateb = sb("gateb", [P, 1, E])
        w1s = sb("w1s", [128, E, H])
        w1_h, w1_l = sb("w1_h", [128, E, H], F32R), sb("w1_l", [128, E, H], F32R)
        b1s = sb("b1s", [H, E])
        w2s = sb("w2s", [H, E, C])
        w2_hl = sb("w2_hl", [H, E, 2, C], F32R)
        b2s = sb("b2s", [LO + E, C])
        b2_h, b2_l = sb("b2_h", [LO + E, C], F32R), sb("b2_l", [LO + E, C], F32R)
        picker = sb("picker", [LO + E, E, H], F32R)
        hankel = sb("hankel", [P, ZW])

        xr = sb("xr", [128, 2, NT, 2, C])
        xT = sb("xT", [128, 2, NP])
        qbuf, kbuf = sb("qbuf", [128, 2, QKW]), sb("kbuf", [128, 2, QKW])
        ts = sb("ts", [128, 2, RC, TW])
        th, tl = sb("th", [128, 2, RC, TW + 1], F32R), sb("tl", [128, 2, RC, TW + 1], F32R)
        frow = sb("frow", [4 * WIN, NP])
        mx = sb("mx", [P, 2, 2 * NT])
        es = sb("es", [P, 2, 2 * NT, WIN])
        rs = sb("rs", [P, 2, 2 * NT])
        aw = sb("aw", [P, 2 * NT, GROUPS_T * WIN])
        awT = sb("awT", [P, 2, NT, P])
        awE = sb("awE", [TAIL, 2, NT - 1, P])
        h0 = sb("h0", [P, B, NT, C])

        st = sb("st", [P, 2, 2 * NT, 6])
        ln = sb("ln", [P, 2, 8, 2 * NT])
        n1 = sb("n1", [P, 2, NT, 2, C])

        hS = sb("hS", [128, B, NP], F32R)
        kS = sb("kS", [128, B, NP], F32R)
        v_hl = sb("v_hl", [P, B, NT, 2, C], F32R)
        sc = sb("sc", [P, 2, NW])
        nmax = sb("nmax", [P, 2])
        pr = xT[0:P, :, :]
        rsum, rinv = sb("rsum", [P, NT]), sb("rinv", [P, NT])
        pT_h, pT_l = sb("pT_h", [P, 2, NP], F32R), sb("pT_l", [P, 2, NP], F32R)
        ob, ol = (qbuf[0:P, n, 0:2 * NT * C].rearrange("p (b i c) -> p b i c", b=2, i=NT) for n in range(2))
        st2, st3 = sb("st2", [P, NT, 6]), sb("st3", [P, NT, 6])
        ln2, ln3 = sb("ln2", [P, 8, NT]), sb("ln3", [P, 8, NT])
        h1 = xr[0:P, :, :, :, :].rearrange("p j i h c -> p (j i h c)")\
            .rearrange("p (b i c) -> p b i c", b=B, c=C)
        n3 = [n1[:, n % 2, :, :, :] for n in range(B)]
        pt = sb("pt", [P, 6, NT, E])
        pm = sb("pm", [P, 4, NT])
        cws = sb("cws", [P, NT, E])

        pick_f = sc[0:LO + E, :, :].rearrange("p a m -> p (a m)")[:, 0:E * H].rearrange("p (e h) -> p e h", e=E)

        nS = hS
        flat = "p a r n -> p (a r n)"
        ts_f, th_f, tl_f = ts.ap().rearrange(flat), th.ap().rearrange(flat), tl.ap().rearrange(flat)
        cwS = tl_f[0:LO + E, 0:B * NP]
        qH = th_f[:, 0:B * NP].rearrange("p (b n) -> p b n", b=B)
        qL = [(tl_f if b < 2 else th_f)[:, (B + b % 2) * NP:(B + b % 2 + 1) * NP] for b in range(B)]
        RG, RH = 5, 6
        ge = ts_f[:, 0:RG * HALF].rearrange("p (k n) -> p k n", k=RG)
        gw = ts_f[:, RG * HALF:2 * RG * HALF].rearrange("p (k n) -> p k n", k=RG)
        ysb = ts_f[:, 2 * RG * HALF:(2 * RG + 2) * HALF].rearrange("p (k n) -> p k n", k=2)
        gh = th_f[:, 0:RH * HALF].rearrange("p (k n) -> p k n", k=RH)
        gl = th_f[:, RH * HALF:2 * RH * HALF].rearrange("p (k n) -> p k n", k=RH)
        yo = h0
        HI_DVE = [(3,)] * (2 * B - 2) + [(2, 5)] * 2

        x_in = [sem("x_in0"), sem("x_in1")]
        xrow_in, tokw_in, attw_in, ffnw_in = sem("xrow_in"), sem("tokw_in"), sem("attw_in"), sem("ffnw_in")
        ext_out, hankel_in, stored = sem("ext_out"), sem("hankel_in"), sem("stored")
        pad_set, blank_set, ident_set, const_set, edge_set, mask_step, b2_blank = (
            sem("pad_set"), sem("blank_set"), sem("ident_set"), sem("const_set"), sem("edge_set"),
            sem("mask_step"), sem("b2_blank"))
        prep_dve, prep_mm, prep_act, prep_pool = sem("prep_dve"), sem("prep_mm"), sem("prep_act"), sem("prep_pool")
        qk_mm, k_ev, q_ev = sem("qk_mm"), sem("k_ev"), sem("q_ev")
        sum_dve, sum_pool, tanh_h, tanh_f, tl_dve, f_mm = (
            sem("sum_dve"), sem("sum_pool"), sem("tanh_h"), sem("tanh_f"), sem("tl_dve"), sem("f_mm"))
        smax_chain, shifted, wexp, aw_done = sem("smax_chain"), sem("shifted"), sem("wexp"), sem("aw_done")
        f_copied, fT_mm, h0_off, s2_pow, s3_pow = (
            sem("f_copied"), sem("fT_mm"), sem("h0_off"), sem("s2_pow"), sem("s3_pow"))
        n3T_mm, lg_mm, lg_read, cwT_mm, b2_mm = sem("n3T_mm"), sem("lg_mm"), sem("lg_read"), sem("cwT_mm"), sem("b2_mm")
        tokv_in, tanh_w = sem("tokv_in"), sem("tanh_w")
        n1_even, n1_odd = sem("n1_even"), sem("n1_odd")
        awT_mm, awT_ev, tok_mm, ln1_chain, h0_out, ln1_var, ln1_pow = (
            sem("awT_mm"), sem("awT_ev"), sem("tok_mm"), sem("ln1_chain"), sem("h0_out"), sem("ln1_var"),
            sem("ln1_pow"))
        hT_mm, hS_h, hS_l, k_mm, kS_h, kS_l, v_mm, v_h, v_l = (
            sem("hT_mm"), sem("hS_h"), sem("hS_l"), sem("k_mm"), sem("kS_h"), sem("kS_l"), sem("v_mm"),
            sem("v_h"), sem("v_l"))
        q_mm, q_h, q_l, s_mm, s_max, p_done = (sem("q_mm"), sem("q_h"), sem("q_l"), sem("s_mm"),
                                               sem("s_max"), sem("p_done"))
        pT_mm, pT_hi, pT_lo, pv_mm = sem("pT_mm"), sem("pT_hi"), sem("pT_lo"), sem("pv_mm")
        rinv_done, o_read, o_bias, var2, h1_done, var3, n3_done = (
            sem("rinv_done"), sem("o_read"), sem("o_bias"), sem("var2"), sem("h1_done"), sem("var3"),
            sem("n3_done"))
        pool_chain, post_dve, nS_h, nS_l, lg_shift, lg_exp, cw_done, cw_h, cw_l, base_done = (
            sem("pool_chain"), sem("post_dve"), sem("nS_h"), sem("nS_l"), sem("lg_shift"),
            sem("lg_exp"), sem("cw_done"), sem("cw_h"), sem("cw_l"), sem("base_done"))
        up_mm, cb_mm, gelu_done, gw_done, gh_act, gh_dve, gl_pool, gl_dve, down_mm = (
            sem("up_mm"), sem("cb_mm"), sem("gelu_done"), sem("gw_done"), sem("gh_act"), sem("gh_dve"),
            sem("gl_pool"), sem("gl_dve"), sem("down_mm"))
        y_copied, yT_mm, y_add, y_sum = sem("y_copied"), sem("yT_mm"), sem("y_add"), sem("y_sum")

        TOKW, ATTW, FFNW = 4 * 16, 12 * 16, 13 * 16
        REST = L - (NT - 1) * P
        KCH = 2 * (WIN // RC)
        KC = 2 * B * E
        block = ctx.enter_context(nc.Block())

        S0 = B * NT

        def x(*slots):
            return tuple(S0 + n for n in slots)

        PE_POST = by_slot((13.5, 14.5, 15.5, 20.5, 21.5, 23), (19, 20, 21) + x(5, 7, 9), x(11, 13, 15, 27, 29, 36),
                          x(26, 31, 33, 44, 46, 49))
        ACT_POST = by_slot((14, 15, 17, 21, 22), (19, 20, 22) + x(6, 8), x(12, 14, 18, 28, 30),
                           x(27, 32, 36, 45, 47))
        DVE_POST = by_slot((7, 8, 8, 8, 8, 11, 11, 11, 11, 11, 15, 16, 17, 17, 17) + (18,) * 5 + (19,) * 5 + (20,) * 6
                           + (22, 23, S0 + 1),
                           (13, 14, 14, 14, 14, 16, 17, 17, 17, 17, 20, 21, 22, 22, 22) + (23,) * 4
                           + x(0) * 3 + x(1) * 3 + x(2) * 3 + x(3) * 3 + x(6, 8, 10),
                           (19, 20, 20, 20, 20, 23) + x(0, 0, 0, 0, 12, 14, 16, 16, 17)
                           + x(*(n for n in range(18, 26) for _ in range(2))) + x(28, 30, 37),
                           x(8, 9, 9, 10, 10, 18, 19, 19, 20, 20, 27, 32, 34, 34, 35)
                           + x(*(n for n in range(36, 44) for _ in range(2))) + x(45, 47, 50))
        POOL_POST = by_slot((), (), (0, 0, 0, 0) + x(0, 0, 0), x(5, 9, 11, 13, 20, 21, 22))
        assert all(sum(p[0] == b for ps in DVE_POST.values() for p in ps) == 34 for b in range(B))

        def halves(bank, rows=128):
            return ps[0:rows, bank:bank + 2, 0:HALF]

        def cols(t):
            return t.rearrange("p (h n) -> p h n", h=2)

        def n_dve(k):
            return sum(m % E in HI_DVE[m // E] for m in range(k))

        @block.sync
        def _(sp):
            def col(t):
                return t.rearrange("(c a) -> c a", a=1)

            sp.wait_ge(pad_set, 1)
            sp.dma_start(xT[:, 0, 0:L], xcol[0]).then_inc(x_in[0], 16)
            sp.wait_ge(blank_set, 1)
            for hf in range(2):
                rows = slice(C * hf, C * hf + C)
                sp.dma_start(wk2[rows, rows], w_key).then_inc(tokw_in, 16)
                sp.dma_start(wq2[rows, rows], w_qry).then_inc(tokw_in, 16)
            for hf in range(2):
                rows = slice(C * hf, C * hf + C)
                sp.dma_start(tokb[rows, :], col(tok_b)).then_inc(tokv_in, 16)
                sp.dma_start(v2[rows, hf:hf + 1], col(tok_v)).then_inc(tokv_in, 16)
            sp.dma_start(xT[:, 1, 0:L], xcol[1]).then_inc(x_in[1], 16)
            for hf in range(2):
                rows = slice(C * hf, C * hf + C)
                sp.dma_start(gcol[rows, :], col(ln1_g)).then_inc(attw_in, 16)
                sp.dma_start(bcol[rows, :], col(ln1_b)).then_inc(attw_in, 16)
                for n in range(2):
                    sp.dma_start(qkb[rows, n:n + 1], col(qkv_b[C * n:C * n + C])).then_inc(attw_in, 16)
                sp.dma_start(wqkv[rows, :], qkv_w).then_inc(attw_in, 16)
            sp.dma_start(bvc[:, :], col(qkv_b[2 * C:3 * C])).then_inc(attw_in, 16)
            sp.dma_start(wproj[:, :], proj_w).then_inc(attw_in, 16)
            sp.wait_ge(pad_set, 2)
            for b in range(B):
                j, hf = b // 2, b % 2
                sp.dma_start(xr[0:P, j, 0:NT - 1, hf, :],
                             xrow[b, 0:(NT - 1) * P, :].rearrange("(i p) c -> p i c", p=P)).then_inc(xrow_in, 16)
                sp.dma_start(xr[0:REST, j, NT - 1, hf, :], xrow[b, (NT - 1) * P:L, :]).then_inc(xrow_in, 16)
            sp.dma_start(scalec[:, :], bass.AP(scale.tensor, 0, [[0, 128], [1, 1]])).then_inc(ffnw_in, 16)
            sp.dma_start(bass.AP(table_ext, 0, [[1, LEAD], [1, 1]]),
                         bass.AP(rtable.tensor, 0, [[0, LEAD], [1, 1]])).then_inc(ext_out, 16)
            sp.dma_start(table_ext.ap()[LEAD:LEAD + TABLE], rtable).then_inc(ext_out, 16)
            rest = EXT - LEAD - TABLE
            sp.dma_start(table_ext.ap()[LEAD + TABLE:EXT], rtable[0:rest]).then_inc(ext_out, 16)
            for dst, src, n in ((projb, proj_b, C), (g2b, ln2_g, C), (b2b, ln2_b, C), (gateb, gate_b, E)):
                sp.dma_start(dst[:, 0, :], bass.AP(src.tensor, 0, [[0, P], [1, n]])).then_inc(ffnw_in, 16)
            sp.wait_ge(ext_out, 48)
            sp.dma_start(hankel[:, :], bass.AP(table_ext, 0, [[1, P], [1, ZW]])).then_inc(hankel_in, 16)
            for hf in range(2):
                rows = slice(C * hf, C * hf + C)
                sp.dma_start(gatew[rows, :], gate_w).then_inc(ffnw_in, 16)
                sp.dma_start(w1s[rows, :, :], w1.rearrange("e c h -> c e h")).then_inc(ffnw_in, 16)
            sp.dma_start(b1s[:, :], b1).then_inc(ffnw_in, 16)
            sp.dma_start(w2s[:, :, :], w2.rearrange("e h c -> h e c")).then_inc(ffnw_in, 16)
            sp.wait_ge(b2_blank, 1)
            for r0 in (0, LO):
                sp.dma_start(b2s[r0:r0 + E, :], b2).then_inc(ffnw_in, 16)
            for b in range(B):
                sp.wait_ge(y_sum, 2 * (b + 1))
                sp.dma_start(out[b, 0:(NT - 1) * P, :].rearrange("(i p) c -> p i c", p=P),
                             yo[0:P, b, 0:NT - 1, :]).then_inc(stored, 16)
                sp.dma_start(out[b, (NT - 1) * P:NW, :], yo[0:NW - (NT - 1) * P, b, NT - 1, :]).then_inc(stored, 16)
            sp.wait_ge(stored, 32 * B)

        def add_window(eng, k, r):
            j, res = k // (WIN // RC), RC * (k % (WIN // RC)) + r
            q = qbuf[:, j, res:res + TW].rearrange("p (g i) -> p g i", i=WIN)
            key = kbuf[:, j, res:res + TW].rearrange("p (g i) -> p g i", i=WIN)[:, :, 0:1]
            return eng.tensor_tensor(ts[:, k % 2, r, :].rearrange("p (g i) -> p g i", i=WIN), q,
                                     key.to_broadcast([128, GROUPS, WIN]), ALU.add)

        RP = RC - 1

        @block.gpsimd
        def _(pool):
            nc.gpsimd.memset(wk2[:, :], 0.0)
            nc.gpsimd.memset(wq2[:, :], 0.0)
            nc.gpsimd.memset(v2[:, :], 0.0).then_inc(blank_set, 1)
            nc.gpsimd.memset(ident[:, :], 0.0).then_inc(mask_step, 1)
            nc.gpsimd.memset(band[:, :, :], 1.0).then_inc(mask_step, 1)
            nc.gpsimd.memset(pick_f, 0.0).then_inc(mask_step, 1)
            pool.wait_ge(mask_step, 3)
            nc.gpsimd.affine_select(out=ident[:, :], in_=ident[:, :], compare_op=ALU.not_equal, fill=1.0, base=0,
                                    pattern=[[-1, 128]], channel_multiplier=1).then_inc(ident_set, 1)
            bandf = band[:, :, :].rearrange("p g r -> p (g r)")
            nc.gpsimd.affine_select(out=bandf, in_=bandf, compare_op=ALU.is_ge, fill=0.0, base=0,
                                    pattern=[[1, GROUPS_T * WIN]], channel_multiplier=-1)
            nc.gpsimd.affine_select(out=pick_f, in_=pick_f, compare_op=ALU.not_equal, fill=1.0, base=0,
                                    pattern=[[-1, E], [0, H]], channel_multiplier=1).then_inc(mask_step, 1)
            pool.wait_ge(mask_step, 4)
            nc.gpsimd.affine_select(out=bandf, in_=bandf, compare_op=ALU.is_ge, fill=0.0, base=TAIL,
                                    pattern=[[-1, GROUPS_T * WIN]], channel_multiplier=1)
            nc.gpsimd.affine_select(out=pick_f, in_=pick_f, compare_op=ALU.not_equal, fill=1.0, base=-LO,
                                    pattern=[[-1, E], [0, H]], channel_multiplier=1).then_inc(mask_step, 1)
            for e in range(E):
                nc.gpsimd.memset(rank[:, e:e + 1], float(E - e))
            nc.gpsimd.memset(half_neg[:, :], -0.5).then_inc(const_set, 1)
            pool.wait_ge(mask_step, 5)
            nc.gpsimd.tensor_copy(picker[:, :, :], pick_f).then_inc(prep_pool, 1)

            for k in range(KCH):
                j = k // (WIN // RC)
                pool.wait_ge(k_ev, j + 1)
                pool.wait_ge(q_ev, j + 1)
                if k >= 2:
                    pool.wait_ge(tl_dve, k - 1)
                add_window(nc.gpsimd, k, RP).then_inc(sum_pool, 1)

            def split(hi, lo, src, after=None):
                nc.gpsimd.tensor_copy(hi, src).then_inc(prep_pool, 1)
                n[0] += 1
                pool.wait_ge(prep_pool, n[0])
                nc.gpsimd.tensor_tensor(lo, src, f32(hi), ALU.subtract)

            n = [1]
            pool.wait_ge(const_set, 1)
            for j in range(2):
                pool.wait_ge(ln1_var, j + 1)
                w = ln[:, j, :, :]
                nc.gpsimd.tensor_tensor(w[:, 5, :], w[:, 4, :], half_neg[:, :], ALU.pow).then_inc(ln1_pow, 1)
                pool.wait_ge(ln1_pow, 2 * j + 1)
                nc.gpsimd.tensor_tensor(w[:, 6, :], w[:, 0, :], w[:, 5, :], ALU.mult).then_inc(ln1_pow, 1)
                if j == 0:
                    pool.wait_ge(ffnw_in, FFNW)
                    split(gate_h[:, :], gate_l[:, :], gatew[:, :])
                    split(b2_h[:, :], b2_l[:, :], b2s[:, :])
                    split(w2_hl[:, :, 0, :], w2_hl[:, :, 1, :], w2s[:, :, :])
            for half in (slice(0, E // 2), slice(E // 2, E)):
                split(w1_h[:, half, :], w1_l[:, half, :], w1s[:, half, :])
            nc.gpsimd.memset(f32(cwS[:, :]), 0.0).then_inc(prep_pool, 1)
            pool.wait_ge(n1_even, 2)
            pool.wait_ge(n1_odd, 2)
            for b in range(B):
                nc.gpsimd.tensor_tensor(h0[:, b, :, :], h0[:, b, :, :], b2b[:, :, :].to_broadcast([P, NT, C]),
                                        ALU.add).then_inc(h0_off, 1)
            pool.wait_ge(h0_off, B)

            links = [0]

            def link(ins):
                links[0] += 1
                ins.then_inc(pool_chain, 1)
                pool.wait_ge(pool_chain, links[0])

            def post(b, part):
                def wide(t):
                    return t[:, :, :].to_broadcast([P, NT, C])

                def rows(t):
                    return t.unsqueeze(2).to_broadcast([P, NT, C])

                o = ob[:, b % 2, :, :]
                if part == 0:
                    pool.wait_ge(o_read, 2 * b + 2)
                    link(nc.gpsimd.tensor_tensor(o, o, ol[:, b % 2, :, :], ALU.add))
                    nc.gpsimd.tensor_tensor(o, o, wide(projb), ALU.add).then_inc(o_bias, 1)
                if part == 1:
                    pool.wait_ge(var2, b + 1)
                    link(nc.gpsimd.tensor_tensor(ln2[:, 5, :], ln2[:, 4, :], half_neg[:, 0:NT], ALU.pow))
                    nc.gpsimd.tensor_tensor(ln2[:, 6, :], ln2[:, 0, :], ln2[:, 5, :], ALU.mult).then_inc(s2_pow, 1)
                if part == 2:
                    pool.wait_ge(s2_pow, b + 1)
                    link(nc.gpsimd.tensor_tensor(o, o, rows(ln2[:, 5, :]), ALU.mult))
                    link(nc.gpsimd.tensor_tensor(o, o, rows(ln2[:, 6, :]), ALU.add))
                if part == 3:
                    link(nc.gpsimd.tensor_tensor(o, o, wide(g2b), ALU.mult))
                    nc.gpsimd.tensor_tensor(h1[:, b, :, :], o, h0[:, b, :, :], ALU.add).then_inc(h1_done, 1)
                if part == 4:
                    pool.wait_ge(var3, b + 1)
                    link(nc.gpsimd.tensor_tensor(ln3[:, 5, :], ln3[:, 4, :], half_neg[:, 0:NT], ALU.pow))
                    nc.gpsimd.tensor_tensor(ln3[:, 6, :], ln3[:, 0, :], ln3[:, 5, :], ALU.mult).then_inc(s3_pow, 1)
                if part == 5:
                    pool.wait_ge(s3_pow, b + 1)
                    link(nc.gpsimd.tensor_tensor(o, h1[:, b, :, :], rows(ln3[:, 5, :]), ALU.mult))
                if part == 6:
                    at_least(pool, n3T_mm, 2 * (b - 1))
                    twice = [P, NT, 2, C]
                    nc.gpsimd.tensor_tensor(n3[b], o.unsqueeze(2).to_broadcast(twice),
                                            ln3[:, 6, :].unsqueeze(2).unsqueeze(3).to_broadcast(twice),
                                            ALU.add).then_inc(n3_done, 1)

            for b, parts in ((0, (0, 1, 2, 3)), (1, (0,)), (0, (4, 5, 6)), (1, (1, 2, 3)), (2, (0,)),
                             (1, (4, 5, 6)), (2, (1, 2, 3))):
                for part in parts:
                    post(b, part)

            for k in range(KC):
                for b, part in POOL_POST.get(S0 + k, ()):
                    post(b, part)
                if k % E not in HI_DVE[k // E]:
                    pool.wait_ge(gh_act, k + 1 - n_dve(k + 1))
                    at_least(pool, down_mm, k - RH + 1)
                    nc.gpsimd.tensor_tensor(gl[:, k % RH, :], gw[:, k % RG, :], f32(gh[:, k % RH, :]),
                                            ALU.subtract).then_inc(gl_pool, 1)

        @block.vector
        def _(dve):
            nc.vector.memset(xT[:, :, L:NP], 0.0).then_inc(pad_set, 1)
            nc.vector.memset(xr[EDGE:128, :, NT - 1, :, :], 0.0).then_inc(pad_set, 1)
            nc.vector.memset(b2s[:, :], 0.0).then_inc(b2_blank, 1)
            nc.vector.memset(f32(v9[:, :, :, :, :]), 0.0)
            nc.vector.memset(v9f[:, :, :, :, :], 0.0)
            for j in range(2):
                nc.vector.memset(qbuf[:, j, 0:4], 0.0)
                nc.vector.memset(qbuf[:, j, 4 + NP:QKW], 0.0)
                if j == 1:
                    nc.vector.memset(kbuf[:, j, NP:QKW], 0.0)
            nc.vector.memset(awE[:, :, :, 0:EDGE], 0.0)
            nc.vector.memset(kbuf[:, 0, NP:QKW], 0.0).then_inc(edge_set, 1)
            dve.wait_ge(edge_set, 1)
            dve.wait_ge(tokv_in, TOKW)
            nine = [128, WIN, 2]
            v_high, v_low = (bass.AP(v9, 2 * n, [[4 * WIN * WIN, 128], [4 * WIN + 4, WIN], [1, 2]]) for n in range(2))
            nc.vector.tensor_copy(bass.AP(v9f, 0, [[4 * WIN * WIN, 128], [4 * WIN + 4, WIN], [1, 2]]),
                                  v2[:, :].unsqueeze(1).to_broadcast(nine))
            nc.vector.tensor_copy(v_high, v2[:, :].unsqueeze(1).to_broadcast(nine)).then_inc(prep_dve, 1)
            dve.wait_ge(prep_dve, 1)
            nc.vector.tensor_tensor(v_low, v2[:, :].unsqueeze(1).to_broadcast(nine), f32(v_high),
                                    ALU.subtract).then_inc(prep_dve, 1)

            def queries(j):
                dve.wait_ge(qk_mm, j + 1)
                nc.vector.tensor_scalar(cols(qbuf[:, j, 4:4 + NP]), halves(6), tokb[:, 0:1], None,
                                        ALU.add).then_inc(q_ev, 1)

            def weights():
                dve.wait_ge(attw_in, ATTW)
                w = wqkv[:, 0:2 * C].rearrange("p (n c) -> p n c", n=2).unsqueeze(2).to_broadcast([128, 2, 2, C])
                nc.vector.tensor_scalar(wqk[:, :, :, :], w, gcol[:, 0:1], None, ALU.mult).then_inc(prep_dve, 1)
                dve.wait_ge(prep_dve, 3)
                flat_w = wqk[:, :, :, :].rearrange("p n d c -> p n (d c)")
                nc.vector.tensor_copy(wqk_h[:, :, :], flat_w).then_inc(prep_dve, 1)
                dve.wait_ge(prep_dve, 4)
                nc.vector.tensor_tensor(wqk_l[:, :, :], flat_w, f32(wqk_h[:, :, :]),
                                        ALU.subtract).then_inc(prep_dve, 1)

            def weights_out():
                dve.wait_ge(prep_mm, 3)
                dve.wait_ge(prep_act, 1)
                nc.vector.tensor_tensor(qkc[:, :], ps[:, 6, 0:2], qkb[:, :], ALU.add).then_inc(prep_dve, 1)
                nc.vector.tensor_tensor(tvc[:, :], ps[0:C, 6, 2:3], bvc[:, :], ALU.add).then_inc(prep_dve, 1)

            def values_folded():
                dve.wait_ge(prep_mm, 4)
                dve.wait_ge(ffnw_in, FFNW)
                nc.vector.tensor_scalar(wvp[:, :], ps[:, 6, 128:128 + C], gcol[:, 0:1], scalec[:, 0:1], ALU.mult,
                                        ALU.mult).then_inc(prep_dve, 1)
                dve.wait_ge(prep_dve, 8)
                nc.vector.tensor_copy(wvp_h[:, :], wvp[:, :]).then_inc(prep_dve, 1)
                dve.wait_ge(prep_dve, 9)
                nc.vector.tensor_tensor(wvp_l[:, :], wvp[:, :], f32(wvp_h[:, :]), ALU.subtract).then_inc(prep_dve, 1)
                nc.vector.scalar_tensor_tensor(out=projb[:, 0, :], in0=ps[0:P, 6, 256:256 + C],
                                               scalar=scalec[0:P, 0:1], in1=projb[:, 0, :], op0=ALU.mult,
                                               op1=ALU.add).then_inc(prep_dve, 1)

            def window_softmax(j):
                f = ps[0:P, 4 + j, 0:NT * WIN * 4].rearrange("p (i r l h) -> p i r l h", r=WIN, l=2, h=2)
                e = es[:, j, :, :].rearrange("p (h i) r -> p h i r", h=2)
                dve.wait_ge(fT_mm, j + 1)
                for h in range(2):
                    ins = nc.vector.tensor_reduce(e[:, h, :, :], f[:, :, :, :, h], AX.X, ALU.add)
                ins.then_inc(smax_chain, 1)
                dve.wait_ge(smax_chain, 4 * j + 1)
                nc.vector.tensor_reduce(mx[:, j, :], es[:, j, :, :], AX.X, ALU.max).then_inc(smax_chain, 1)
                dve.wait_ge(smax_chain, 4 * j + 2)
                nc.vector.tensor_tensor(es[:, j, :, :], es[:, j, :, :],
                                        mx[:, j, :].unsqueeze(2).to_broadcast([P, 2 * NT, WIN]),
                                        ALU.subtract).then_inc(shifted, 1)

            def window_weights(j):
                dve.wait_ge(wexp, j + 1)
                if j == 0:
                    dve.wait_ge(const_set, 1)
                else:
                    dve.wait_ge(awT_mm, 2)
                for h in range(2):
                    ins = nc.vector.tensor_tensor(
                        aw[:, NT * h:NT * h + NT, :].rearrange("p t (g r) -> p t g r", r=WIN),
                        es[:, j, NT * h:NT * h + NT, :].unsqueeze(2).to_broadcast([P, NT, GROUPS_T, WIN]),
                        band[:, :, :].unsqueeze(1).to_broadcast([P, NT, GROUPS_T, WIN]), ALU.mult)
                    ins.then_inc(aw_done, 1)
                nc.vector.tensor_reduce(mx[:, j, :], es[:, j, :, :], AX.X, ALU.add).then_inc(smax_chain, 1)
                dve.wait_ge(smax_chain, 4 * j + 3)
                nc.vector.reciprocal(rs[:, j, :], mx[:, j, :]).then_inc(smax_chain, 1)
                dve.wait_ge(smax_chain, 4 * j + 4)

            queries(0)
            for k in range(KCH + 1):
                if k < KCH:
                    j = k // (WIN // RC)
                    dve.wait_ge(k_ev, j + 1)
                    dve.wait_ge(q_ev, j + 1)
                    if k >= 2:
                        dve.wait_ge(f_mm, k - 1)
                    for r in range(RP):
                        add_window(nc.vector, k, r).then_inc(sum_dve, 1)
                if k == KCH - 1:
                    window_softmax(0)
                if k == 0:
                    queries(1)
                    nc.vector.memset(pr[:, :, NW:NP], 0.0).then_inc(edge_set, 1)
                    weights()
                if k >= 1:
                    dve.wait_ge(tanh_f, k)
                    dve.wait_ge(tanh_h, k)
                    at_least(dve, f_mm, k - 2)
                    n = (k - 1) % 2
                    nc.vector.tensor_tensor(tl[:, n, RP, 0:TW], ts[:, n, RP, :], f32(th[:, n, RP, 0:TW]),
                                            ALU.subtract).then_inc(tl_dve, 1)
                if k == 2:
                    weights_out()
                if k == KCH // 2 + 1:
                    values_folded()
                if k == KCH // 2 + 2:
                    window_weights(0)
            window_softmax(1)

            def row_moments(part, chain, src, stats, w, var_scale, eps):
                if part == 0:
                    for i in range(stats.shape[1]):
                        ins = nc.vector.bn_stats(stats[:, i, :], src[:, i, :])
                if part == 1:
                    nc.vector.tensor_tensor(w[:, 7, :], stats[:, :, 1], stats[:, :, 4], ALU.add)
                    nc.vector.tensor_tensor(w[:, 2, :], stats[:, :, 2], stats[:, :, 5], ALU.add)
                    ins = nc.vector.tensor_tensor(w[:, 1, :], stats[:, :, 1], stats[:, :, 4], ALU.subtract)
                if part == 2:
                    nc.vector.tensor_scalar(w[:, 0, :], w[:, 7, :], -0.5, None, ALU.mult)
                    ins = nc.vector.tensor_tensor(w[:, 3, :], w[:, 1, :], w[:, 1, :], ALU.mult)
                if part == 3:
                    ins = nc.vector.scalar_tensor_tensor(out=w[:, 3, :], in0=w[:, 3, :], scalar=C / 4.0,
                                                         in1=w[:, 2, :], op0=ALU.mult, op1=ALU.add)
                if part == 4:
                    return nc.vector.tensor_scalar(w[:, 4, :], w[:, 3, :], var_scale, eps, ALU.mult, ALU.add)
                return chain(ins)

            lc = [0]

            def ln1_link(ins):
                lc[0] += 1
                ins.then_inc(ln1_chain, 1)
                dve.wait_ge(ln1_chain, lc[0])

            def first_rows(j):
                for hf in range(2):
                    b = 2 * j + hf
                    dve.wait_ge(tok_mm, b + 1)
                    o = ps[0:P, hf, 0:NT * C].rearrange("p (i c) -> p i c", c=C)
                    r = rs[:, j, NT * hf:NT * hf + NT].unsqueeze(2).to_broadcast([P, NT, C])
                    nc.vector.tensor_tensor(h0[:, b, :, :], o, r, ALU.mult).then_inc(h0_out, 1)

            def first_moments(j):
                dve.wait_ge(h0_out, 2 * j + 2)
                rows = h0[:, 2 * j:2 * j + 2, :, :].rearrange("p b i c -> p (b i) c")
                for part in range(5):
                    ins = row_moments(part, ln1_link, rows, st[:, j, :, :], ln[:, j, :, :], (1.0 + EPS) / C, EPS * EPS)
                ins.then_inc(ln1_var, 1)

            def row_split(b):
                t = 4 + 2 * (b % 2)
                dve.wait_ge(hS_h, b + 1)
                nc.vector.tensor_tensor(cols(hS[C:128, b, :]), ps[C:128, t:t + 2, 0:HALF], cols(f32(hS[C:128, b, :])),
                                        ALU.subtract).then_inc(hS_l, 1)

            def first_splits(b):
                def values_low():
                    dve.wait_ge(v_h, b + 1)
                    v = ps[0:P, 4 + 2 * (b % 2), 0:NT * C].rearrange("p (i c) -> p i c", c=C)
                    nc.vector.tensor_tensor(v_hl[:, b, :, 1, :], v, f32(v_hl[:, b, :, 0, :]),
                                            ALU.subtract).then_inc(v_l, 1)

                if b < B - 2:
                    values_low()
                dve.wait_ge(kS_h, b + 1)
                nc.vector.scalar_tensor_tensor(out=cols(kS[C:128, b, :]), in0=ps[C:128, 2:4, 0:HALF],
                                               scalar=qkc[C:128, 1:2], in1=cols(f32(kS[C:128, b, :])),
                                               op0=ALU.add, op1=ALU.subtract).then_inc(kS_l, 1)
                dve.wait_ge(q_h, b + 1)
                nc.vector.scalar_tensor_tensor(out=cols(qL[b]), in0=halves(0), scalar=qkc[:, 0:1],
                                               in1=cols(f32(qH[:, b, :])), op0=ALU.add,
                                               op1=ALU.subtract).then_inc(q_l, 1)
                if b >= B - 2:
                    values_low()

            def normalize(b):
                j = b // 2
                dve.wait_ge(ln1_pow, 2 * j + 2)
                at_least(dve, hT_mm, b - 1)
                for i in range(NT):
                    ins = nc.vector.tensor_scalar(n1[:, 0, i, :, :], h0[:, b, i, :].unsqueeze(1).to_broadcast([P, 2, C]),
                                                  ln[:, j, 5, i:i + 1], ln[:, j, 6, i:i + 1], ALU.mult, ALU.add)
                ins.then_inc(n1_even, 1)

            window_weights(1)
            first_rows(0)
            first_moments(0)
            first_rows(1)
            normalize(0)
            first_moments(1)
            row_split(0)
            row_split(1)
            normalize(2)
            first_splits(0)
            row_split(2)
            first_splits(1)
            row_split(3)
            first_splits(2)
            first_splits(3)

            dve.wait_ge(hankel_in, 16)
            dve.wait_ge(prep_dve, 11)

            def scores(n):
                i = n % NT
                dve.wait_ge(s_mm, n + 1)
                at_least(dve, p_done, n - 1)
                bias = bass.AP(hankel, P * i + NW - 1, [[ZW, P], [-MH, 2], [-1, MH]])
                s = bass.AP(ps, 2 * (i % 2) * 512, [[8 * 512, P], [513, 2], [1, MH]])
                nc.vector.tensor_tensor_reduce(
                    out=sc[:, i % 2, :].rearrange("p (h m) -> p h m", h=2), in0=s, in1=bias, scale=-1.0, scalar=BIG,
                    op0=ALU.add, op1=ALU.min, accum_out=nmax[:, i % 2:i % 2 + 1]).then_inc(s_max, 1)

            def probs_low(n, h):
                i = n
                at_least(dve, pv_mm, n - 1)
                dve.wait_ge(pT_hi, 2 * n + h + 1)
                c = slice(HALF * h, HALF * h + HALF)
                nc.vector.tensor_tensor(pT_l[:, i % 2, c], ps[0:P, 4 + h, 0:HALF], f32(pT_h[:, i % 2, c]),
                                        ALU.subtract).then_inc(pT_lo, 1)

            def attention_out(n):
                b, g = n // 2, n % 2
                tiles = slice(3 * g, 3 * g + 3)
                dve.wait_ge(p_done, 3 * n + 3)
                nc.vector.reciprocal(rinv[:, tiles], rsum[:, tiles]).then_inc(rinv_done, 1)
                dve.wait_ge(rinv_done, n + 1)
                dve.wait_ge(pv_mm, 3 * n + 3)
                at_least(dve, n3_done, b - 1)
                o = ps[0:P, 6, 0:3 * 2 * C].rearrange("p (i l c) -> p i l c", l=2, c=C)
                r = rinv[:, tiles].unsqueeze(2).to_broadcast([P, 3, C])
                nc.vector.tensor_tensor(ob[:, b % 2, tiles, :], o[:, :, 0, :], r, ALU.mult)
                nc.vector.tensor_tensor(ol[:, b % 2, tiles, :], o[:, :, 1, :], r, ALU.mult).then_inc(o_read, 1)

            links = [0]

            def post(b, part):
                def link(ins):
                    links[0] += 1
                    return ins.then_inc(post_dve, 1)

                def wide(t):
                    return t.unsqueeze(2).to_broadcast([P, NT, E])

                lg, eq, p, s1, s2 = (pt[:, n, :, :] for n in range(5))
                top, total, inv, first = (pm[:, n, :] for n in range(4))
                rk = rank[:, :].unsqueeze(1).to_broadcast([P, NT, E])

                def pick(step, src, sel):
                    if step == 0:
                        link(nc.vector.tensor_reduce(top, src, AX.X, ALU.max))
                    if step == 1:
                        link(nc.vector.tensor_tensor(eq, src, wide(top), ALU.is_equal))
                    if step == 2:
                        link(nc.vector.tensor_tensor(eq, eq, rk, ALU.mult))
                    if step == 3:
                        link(nc.vector.tensor_reduce(first, eq, AX.X, ALU.max))
                    if step == 4:
                        link(nc.vector.tensor_tensor(sel, eq, wide(first), ALU.is_equal))

                at_least(dve, post_dve, links[0])
                if part < 5:
                    if part == 0:
                        dve.wait_ge(o_bias, b + 1)
                    ins = row_moments(part, link, ob[:, b % 2, :, :], st2, ln2, 1.0 / C, EPS)
                    if part == 4:
                        ins.then_inc(var2, 1)
                elif part < 10:
                    if part == 5:
                        dve.wait_ge(h1_done, b + 1)
                    ins = row_moments(part - 5, link, h1[:, b, :, :], st3, ln3, 1.0 / C, EPS)
                    if part == 9:
                        ins.then_inc(var3, 1)
                elif part < 12:
                    h = part - 10
                    dve.wait_ge(nS_h, 2 * b + h + 1)
                    c = slice(HALF * h, HALF * h + HALF)
                    nc.vector.tensor_tensor(nS[C:128, b, c], ps[C:128, 7, 0:HALF], f32(nS[C:128, b, c]),
                                            ALU.subtract).then_inc(nS_l, 1)
                elif part == 12:
                    dve.wait_ge(lg_mm, b + 1)
                    nc.vector.tensor_tensor(lg, ps[0:P, 7, 0:NT * E].rearrange("p (i e) -> p i e", e=E),
                                            gateb[:, :, :].to_broadcast([P, NT, E]), ALU.add).then_inc(lg_read, 1)
                elif part == 13:
                    dve.wait_ge(lg_read, b + 1)
                    link(nc.vector.tensor_reduce(top, lg, AX.X, ALU.max))
                elif part == 14:
                    nc.vector.tensor_tensor(lg, lg, wide(top), ALU.subtract).then_inc(lg_shift, 1)
                elif part == 15:
                    dve.wait_ge(lg_exp, b + 1)
                    link(nc.vector.tensor_reduce(total, lg, AX.X, ALU.add))
                elif part == 16:
                    link(nc.vector.reciprocal(inv, total))
                elif part == 17:
                    link(nc.vector.tensor_tensor(p, lg, wide(inv), ALU.mult))
                elif part < 23:
                    pick(part - 18, p, s1)
                elif part == 23:
                    link(nc.vector.scalar_tensor_tensor(out=lg, in0=s1, scalar=-2.0, in1=p, op0=ALU.mult, op1=ALU.add))
                elif part < 29:
                    pick(part - 24, lg, s2)
                elif part == 29:
                    link(nc.vector.tensor_tensor(s1, s1, s2, ALU.add))
                elif part == 30:
                    nc.vector.tensor_tensor(cws[:, :, :], s1, p, ALU.mult).then_inc(cw_done, 1)
                elif part < 33:
                    h = part - 31
                    dve.wait_ge(cw_h, 2 * b + h + 1)
                    c = slice(NP * b + HALF * h, NP * b + HALF * h + HALF)
                    nc.vector.tensor_tensor(cwS[LO:LO + E, c], ps[0:E, 7, 0:HALF], f32(cwS[0:E, c]),
                                            ALU.subtract).then_inc(cw_l, 1)
                else:
                    dve.wait_ge(b2_mm, b + 1)
                    nc.vector.tensor_tensor(h1[:, b, :, :], ps[0:P, 7, 0:NT * C].rearrange("p (i c) -> p i c", c=C),
                                            h1[:, b, :, :], ALU.add).then_inc(base_done, 1)

            scores(0)
            scores(1)
            for n in range(B * NT):
                if n >= 3 and n % 3 == 0:
                    attention_out(n // 3 - 1)
                parts = DVE_POST.get(n, ())
                late = 2 if len(parts) > 3 and parts[-1][1] >= 15 else 0
                for b, part in parts[:len(parts) - late]:
                    post(b, part)
                probs_low(n, 0)
                for b, part in parts[len(parts) - late:][:1]:
                    post(b, part)
                probs_low(n, 1)
                for b, part in parts[len(parts) - late:][1:]:
                    post(b, part)
                if n + 2 < B * NT:
                    scores(n + 2)
            attention_out(2 * B - 1)

            def y_down(n):
                b, hf = n // 2, n % 2
                tiles = slice(3 * hf, 3 * hf + 3)
                dve.wait_ge(yT_mm, n + 1)
                y = ps[0:P, 6, 0:3 * 128].rearrange("p (t l c) -> p t l c", l=2, c=C)
                nc.vector.tensor_tensor(yo[:, b, tiles, :], y[:, :, 0, :], h1[:, b, tiles, :], ALU.add).then_inc(y_add, 1)
                dve.wait_ge(y_add, n + 1)
                nc.vector.tensor_tensor(yo[:, b, tiles, :], y[:, :, 1, :], yo[:, b, tiles, :], ALU.add).then_inc(y_sum, 1)

            for k in range(KC + 1):
                for b, part in DVE_POST.get(S0 + k, ()):
                    post(b, part)
                if k < KC:
                    dve.wait_ge(gelu_done, k + 1)
                    dve.wait_ge(cb_mm, k + 1)
                    at_least(dve, gl_pool, k - RG + 1 - n_dve(k - RG + 1) if k >= RG else 0)
                    nc.vector.tensor_tensor(gw[:, k % RG, :], ge[:, k % RG, :], ps[:, 2 + k % 2, 0:HALF],
                                            ALU.mult).then_inc(gw_done, 1)
                m = k - 1
                if m >= 0 and m % E in HI_DVE[m // E]:
                    at_least(dve, down_mm, m - RH + 1)
                    dve.wait_ge(gw_done, m + 1)
                    nc.vector.tensor_copy(gh[:, m % RH, :], gw[:, m % RG, :]).then_inc(gh_dve, 1)
                    dve.wait_ge(gh_dve, n_dve(m + 1))
                    nc.vector.tensor_tensor(gl[:, m % RH, :], gw[:, m % RG, :], f32(gh[:, m % RH, :]),
                                            ALU.subtract).then_inc(gl_dve, 1)
                if k % E == 1 and k > 2 * E:
                    y_down(k // E - 2)
            y_down(KC // E - 2)
            y_down(KC // E - 1)

        def y_up(act, n):
            act.wait_ge(down_mm, E * (n + 1))
            at_least(act, yT_mm, n - 1)
            nc.scalar.activation(ysb[:, n % 2, :], ps[:, 4 + n % 2, 0:HALF], ACT.Copy).then_inc(y_copied, 1)

        @block.scalar
        def _(act):
            def keys(j):
                act.wait_ge(qk_mm, j + 1)
                if j == 0:
                    act.wait_ge(edge_set, 1)
                nc.scalar.activation(cols(kbuf[:, j, 0:NP]), halves(4), ACT.Copy).then_inc(k_ev, 1)

            def tanhs(k):
                act.wait_ge(sum_dve, RP * (k + 1))
                whole, last = ts[:, k % 2, 0:RP, :], ts[:, k % 2, RP, :]
                nc.scalar.activation(whole, whole, ACT.Tanh).then_inc(tanh_w, 1)
                act.wait_ge(sum_pool, k + 1)
                at_least(act, f_mm, k - 1)
                nc.scalar.activation(th[:, k % 2, RP, 0:TW], last, ACT.Tanh).then_inc(tanh_h, 1)
                nc.scalar.activation(last, last, ACT.Tanh).then_inc(tanh_f, 1)

            def window_exp(j):
                act.wait_ge(shifted, j + 1)
                nc.scalar.activation(es[:, j, :, :], es[:, j, :, :], ACT.Exp).then_inc(wexp, 1)

            def scores_out(j):
                act.wait_ge(f_mm, (j + 1) * (WIN // RC))
                at_least(act, fT_mm, j)
                nc.scalar.activation(cols(frow[:, :]), halves(2 * j, 4 * WIN), ACT.Copy).then_inc(f_copied, 1)

            keys(0)
            for k in range(KCH):
                tanhs(k)
                if k == 0:
                    keys(1)
                if k == 1:
                    act.wait_ge(prep_mm, 3)
                    nc.scalar.activation(wvt[:, :], ps[0:C, 6, 64:64 + C], ACT.Copy).then_inc(prep_act, 1)
                if k == KCH // 2:
                    scores_out(0)
                if k == KCH // 2 + 1:
                    window_exp(0)

            def weights_up(b):
                act.wait_ge(awT_mm, b + 1)
                at_least(act, tok_mm, b - 1)
                t, n = 6 - 4 * (b % 2), b % 2
                nc.scalar.activation(awT[:, n, :, :].rearrange("p (h i) n -> p h (i n)", h=2), halves(t, P), ACT.Copy)
                nc.scalar.activation(awE[:, n, 0:4, EDGE:P], ps[0:TAIL, t, HALF:HALF + 4 * NE]
                                     .rearrange("p (i n) -> p i n", n=NE), ACT.Copy)
                nc.scalar.activation(awE[:, n, 4, EDGE:P], ps[0:TAIL, t + 1, HALF:HALF + NE],
                                     ACT.Copy).then_inc(awT_ev, 1)

            def normalize(b):
                j, hf = b // 2, b % 2
                act.wait_ge(ln1_pow, 2 * j + 2)
                at_least(act, hT_mm, b - 1)
                for i in range(NT):
                    n = NT * hf + i
                    ins = nc.scalar.activation(n1[:, hf, i, :, :], h0[:, b, i, :].unsqueeze(1).to_broadcast([P, 2, C]),
                                               ACT.Identity, bias=ln[:, j, 6, n:n + 1], scale=ln[:, j, 5, n:n + 1])
                ins.then_inc(n1_odd, 1)

            def row_high(b):
                act.wait_ge(hT_mm, b + 1)
                nc.scalar.activation(cols(hS[:, b, :]), halves(4 + 2 * (b % 2)), ACT.Copy).then_inc(hS_h, 1)

            def high_parts(b):
                act.wait_ge(k_mm, b + 1)
                nc.scalar.activation(cols(kS[:, b, :]), halves(2), ACT.Identity, bias=qkc[:, 1:2]).then_inc(kS_h, 1)
                act.wait_ge(q_mm, b + 1)
                nc.scalar.activation(cols(qH[:, b, :]), halves(0), ACT.Identity, bias=qkc[:, 0:1]).then_inc(q_h, 1)
                act.wait_ge(v_mm, b + 1)
                nc.scalar.activation(v_hl[:, b, :, 0, :], ps[0:P, 4 + 2 * (b % 2), 0:NT * C]
                                     .rearrange("p (i c) -> p i c", c=C), ACT.Copy).then_inc(v_h, 1)

            weights_up(0)
            scores_out(1)
            window_exp(1)
            weights_up(1)
            weights_up(2)
            weights_up(3)
            normalize(1)
            act.wait_ge(prep_dve, 11)
            row_high(0)
            row_high(1)
            high_parts(0)
            normalize(3)
            row_high(2)
            high_parts(1)
            row_high(3)
            high_parts(2)
            high_parts(3)

            def probs(n):
                b, i = n // NT, n % NT
                act.wait_ge(s_max, n + 1)
                at_least(act, pT_mm, 2 * (n - 1))
                if i % 3 == 0:
                    at_least(act, rinv_done, 2 * (b - 1) + i // 3 + 1)
                nc.scalar.activation(pr[:, i % 2, 0:NW], sc[:, i % 2, :], ACT.Exp, bias=nmax[:, i % 2:i % 2 + 1],
                                     scale=-1.0, accum_out=rsum[:, i:i + 1]).then_inc(p_done, 1)

            def probs_high(n):
                i = n
                at_least(act, pv_mm, n - 1)
                for h in range(2):
                    act.wait_ge(pT_mm, 2 * n + h + 1)
                    nc.scalar.activation(pT_h[:, i % 2, HALF * h:HALF * h + HALF], ps[0:P, 4 + h, 0:HALF],
                                         ACT.Copy).then_inc(pT_hi, 1)

            def post(b, part):
                if part < 2:
                    h = part
                    act.wait_ge(n3T_mm, 2 * b + h + 1)
                    nc.scalar.activation(nS[:, b, HALF * h:HALF * h + HALF], ps[:, 7, 0:HALF],
                                         ACT.Copy).then_inc(nS_h, 1)
                if part == 2:
                    act.wait_ge(lg_shift, b + 1)
                    nc.scalar.activation(pt[:, 0, :, :], pt[:, 0, :, :], ACT.Exp).then_inc(lg_exp, 1)
                if part in (3, 4):
                    h = part - 3
                    act.wait_ge(cwT_mm, 2 * b + h + 1)
                    if b == 0 and h == 0:
                        act.wait_ge(prep_pool, 7)
                    nc.scalar.activation(cwS[0:E, NP * b + HALF * h:NP * b + HALF * h + HALF], ps[0:E, 7, 0:HALF],
                                         ACT.Copy).then_inc(cw_h, 1)

            probs(0)
            for n in range(B * NT):
                probs_high(n)
                if n + 1 < B * NT:
                    probs(n + 1)
                for b, part in ACT_POST.get(n, ()):
                    post(b, part)

            HI_LAG = 2
            for k in range(KC + HI_LAG):
                for b, part in ACT_POST.get(S0 + k, ()):
                    post(b, part)
                if k < KC:
                    act.wait_ge(up_mm, k + 1)
                    at_least(act, gw_done, k - RG + 1)
                    nc.scalar.activation(ge[:, k % RG, :], ps[:, k % 2, 0:HALF], ACT.Gelu,
                                         bias=b1s[:, k % E:k % E + 1]).then_inc(gelu_done, 1)
                m = k - HI_LAG
                if m >= 0 and m % E not in HI_DVE[m // E]:
                    act.wait_ge(gw_done, m + 1)
                    at_least(act, down_mm, m - RH + 1)
                    nc.scalar.activation(gh[:, m % RH, :], gw[:, m % RG, :], ACT.Copy).then_inc(gh_act, 1)
                if k % E == 6 and k > E:
                    y_up(act, k // E - 1)
            y_up(act, KC // E - 1)

        @block.tensor
        def _(pe):
            mm, tp = nc.tensor.matmul, nc.tensor.transpose

            def split_mm(o, pairs, start=True, stop=True):
                for n, (a, b) in enumerate(pairs):
                    ins = mm(o, a, b, start=start and n == 0, stop=stop and n == len(pairs) - 1)
                return ins

            def keys_queries(j):
                pe.wait_ge(x_in[j], 16)
                if j == 1:
                    pe.wait_ge(k_ev, 1)
                    pe.wait_ge(q_ev, 1)
                for w, bank in ((wk2, 4), (wq2, 6)):
                    for h in range(2):
                        ins = mm(ps[:, bank + h, 0:HALF], w[:, :], xT[:, j, HALF * h:HALF * h + HALF],
                                 start=True, stop=True)
                ins.then_inc(qk_mm, 1)

            def weights():
                pe.wait_ge(attw_in, ATTW)
                pe.wait_ge(ident_set, 1)
                pe.wait_ge(q_ev, 2)
                w = wqkv[0:C, 0:2 * C].rearrange("p (n c) -> p n c", n=2)
                for n in range(2):
                    for half in (slice(0, C), slice(C, 128)):
                        ins = mm(ps[half, 6, n:n + 1], w[:, n, :], bcol[0:C, :], start=True, stop=True)
                    ins.then_inc(prep_mm, 1)
                mm(ps[0:C, 6, 2:3], wqkv[0:C, 2 * C:3 * C], bcol[0:C, :], start=True, stop=True)
                tp(ps[0:C, 6, 64:64 + C], wqkv[0:C, 2 * C:3 * C], ident[0:C, 0:C]).then_inc(prep_mm, 1)

            def value_weights():
                pe.wait_ge(prep_act, 1)
                pe.wait_ge(prep_dve, 7)
                for half in (slice(0, C), slice(C, 128)):
                    ins = mm(ps[half, 6, 128:128 + C], wvt[:, :], wproj[:, :], start=True, stop=True)
                mm(ps[0:P, 6, 256:256 + C], tvc[:, 0:1].to_broadcast([C, P]), wproj[:, :],
                   start=True, stop=True).then_inc(prep_mm, 1)

            def window_scores(k):
                j, q = k // (WIN // RC), k % (WIN // RC)
                if k == 0:
                    pe.wait_ge(prep_dve, 2)
                for part, (x, v, residues) in enumerate(((ts, v9f, range(RP)), (th, v9, (RP,)), (tl, v9, (RP,)))):
                    if part == 0:
                        pe.wait_ge(tanh_w, k + 1)
                    elif part == 1:
                        pe.wait_ge(tanh_h, k + 1)
                    else:
                        pe.wait_ge(tl_dve, k + 1)
                    for r in residues:
                        res = RC * q + r
                        w = v[:, res, :, :, :].rearrange("p r l h -> p (r l h)")
                        for h in range(2):
                            c0 = HALF * h + TAIL - res
                            ins = mm(ps[0:4 * WIN, 2 * j + h, 0:HALF], w, x[:, k % 2, r, c0:c0 + HALF],
                                     start=(part == 0 and res == 0), stop=(part == 2 and res == WIN - 1))
                ins.then_inc(f_mm, 1)

            def window_rows(j):
                pe.wait_ge(f_copied, j + 1)
                for i in range(NT):
                    m = 4 * WIN * i
                    ins = tp(ps[0:P, 4 + j, m:m + 4 * WIN], frow[:, P * i:P * i + P], ident[0:4 * WIN, 0:4 * WIN])
                ins.then_inc(fT_mm, 1)

            def stay_warm(bank, n):
                for _ in range(n):
                    mm(ps[:, bank, 0:4 * C], wqk_h[:, 0, :], wqk_h[:, :, :].rearrange("p n c -> p (n c)"),
                       start=True, stop=True)

            def window_up(b):
                j, hf = b // 2, b % 2
                pe.wait_ge(aw_done, b + 1)
                if b == 0:
                    pe.wait_ge(prep_dve, 11)
                if b == 1:
                    pe.wait_ge(f_copied, 2)
                at_least(pe, awT_ev, b - 1)
                t = 6 - 4 * (b % 2)
                for i in range(NT):
                    tp(ps[0:P, t + i // 3, P * (i % 3):P * (i % 3) + P], aw[:, NT * hf + i, 0:P], ident[0:P, 0:P])
                for i in range(NT - 1):
                    o = ps[0:TAIL, t + i // 4, HALF + NE * (i % 4):HALF + NE * (i % 4) + NE]
                    ins = tp(o, aw[EDGE:P, NT * hf + i, P:P + TAIL], ident[EDGE:P, EDGE:P])
                ins.then_inc(awT_mm, 1)

            def window_out(b):
                j, hf = b // 2, b % 2
                if b == 1:
                    stay_warm(1, 14)
                pe.wait_ge(awT_ev, b + 1)
                if b == 0:
                    pe.wait_ge(xrow_in, 2 * B * 16)
                if b == 0:
                    pe.wait_ge(f_copied, 1)
                if b >= 2:
                    pe.wait_ge(h0_out, b - 1)
                for i in range(NT):
                    last = i == NT - 1
                    ins = mm(ps[0:P, b % 2, C * i:C * i + C], awT[:, hf, i, :], xr[0:P, j, i, hf, :], start=True,
                             stop=last)
                    if not last:
                        ins = mm(ps[0:P, b % 2, C * i:C * i + C], awE[:, hf, i, :], xr[0:TAIL, j, i + 1, hf, :],
                                 start=False, stop=True)
                ins.then_inc(tok_mm, 1)

            def rows_up(b):
                at_least(pe, v_l, b - 1)
                if b == 0:
                    pe.wait_ge(shifted, 2)
                if b == 1:
                    pe.wait_ge(awT_ev, 3)
                stay_warm(4 + 2 * (b % 2), (10, 0, 3, 3)[b])
                pe.wait_ge(n1_odd if b % 2 else n1_even, b // 2 + 1)
                for i in range(NT):
                    ins = tp(ps[:, 4 + 2 * (b % 2) + i // 3, P * (i % 3):P * (i % 3) + P],
                             n1[:, b % 2, i, :, :].rearrange("p d c -> p (d c)"), ident[0:P, 0:P])
                ins.then_inc(hT_mm, 1)

            def project(b):
                at_least(pe, kS_l, b)
                if b == 0:
                    pe.wait_ge(awT_ev, B)
                    stay_warm(2, 5)
                pe.wait_ge(hS_h, b + 1)
                pe.wait_ge(hS_l, b + 1)
                for n, bank, done in ((1, 2, k_mm), (0, 0, q_mm)):
                    if n == 0:
                        at_least(pe, q_l, b)
                        if b == 0:
                            pe.wait_ge(h0_out, B)
                    for h in range(2):
                        x = hS[:, b, HALF * h:HALF * h + HALF]
                        ins = split_mm(ps[:, bank + h, 0:HALF], [(wqk_h[:, n, :], x), (wqk_l[:, n, :], x)])
                    ins.then_inc(done, 1)
                for i in range(NT):
                    x = hS[:, b, P * i:P * i + P]
                    ins = split_mm(ps[0:P, 4 + 2 * (b % 2), C * i:C * i + C], [(x, wvp_h[:, :]), (x, wvp_l[:, :])])
                ins.then_inc(v_mm, 1)

            pe.wait_ge(tokw_in, TOKW)
            keys_queries(0)
            keys_queries(1)
            for k in range(KCH):
                window_scores(k)
                if k == 0:
                    weights()
                if k == 1:
                    value_weights()
                if k == KCH // 2:
                    window_rows(0)
                if k == KCH // 2 + 1:
                    window_up(0)
            window_out(0)
            window_rows(1)
            window_up(1)
            window_out(1)
            window_up(2)
            window_up(3)
            window_out(2)
            window_out(3)
            rows_up(0)
            rows_up(1)
            for b in range(B):
                project(b)
                if b + 2 < B:
                    rows_up(b + 2)
            stay_warm(5, 6)
            pe.wait_ge(kS_l, B)
            pe.wait_ge(q_l, B)
            pe.wait_ge(v_l, B)

            def scores(n):
                b, i = n // NT, n % NT
                at_least(pe, s_max, n - 1)
                for h in range(2):
                    keys = kS[:, b, (MH - 1) * h:(MH - 1) * h + MH + 1]
                    ins = split_mm(ps[0:P, 2 * (i % 2) + h, 0:MH + 1],
                                   [(qH[:, b, P * i:P * i + P], keys), (qL[b][:, P * i:P * i + P], keys)])
                ins.then_inc(s_mm, 1)

            def probs_up(n):
                i = n
                if n == 0:
                    stay_warm(4, 6)
                pe.wait_ge(p_done, n + 1)
                if n == 0:
                    pe.wait_ge(edge_set, 2)
                at_least(pe, pT_lo, 2 * n)
                for m in range(NT):
                    ins = tp(ps[0:P, 4 + m // 3, P * (m % 3):P * (m % 3) + P], pr[:, i % 2, P * m:P * m + P],
                             ident[0:P, 0:P])
                    if m % 3 == 2:
                        ins.then_inc(pT_mm, 1)

            def values(n):
                b, i = n // NT, n % NT
                if i % 3 == 0:
                    at_least(pe, o_read, n // 3)
                o = ps[0:P, 6, 2 * C * (i % 3):2 * C * (i % 3) + 2 * C]
                for part, (pT, ready) in enumerate(((pT_h, pT_hi), (pT_l, pT_lo))):
                    for m in range(NT):
                        if m % 3 == 0:
                            pe.wait_ge(ready, 2 * n + m // 3 + 1)
                        ins = mm(o, pT[:, i % 2, P * m:P * m + P], v_hl[:, b, m, :, :].rearrange("p l c -> p (l c)"),
                                 start=(part == 0 and m == 0), stop=(part == 1 and m == NT - 1))
                ins.then_inc(pv_mm, 1)

            last_post = []

            def post(b, step):
                if last_post:
                    c, s = last_post[-1]
                    pe.wait_ge(*((nS_l, 2 * c + s + 1), (nS_l, 2 * c + s + 1), (lg_read, c + 1), (cw_l, 2 * c + s - 2),
                                 (cw_l, 2 * c + s - 2), (base_done, c + 1))[s])
                last_post.append((b, step))
                if step < 2:
                    pe.wait_ge(n3_done, b + 1)
                    for i in range(3):
                        ins = tp(ps[:, 7, P * i:P * i + P],
                                 n3[b][:, 3 * step + i, :, :].rearrange("p d c -> p (d c)"), ident[0:P, 0:P])
                    ins.then_inc(n3T_mm, 1)
                elif step == 2:
                    pe.wait_ge(nS_l, 2 * b + 2)
                    if b == 0:
                        pe.wait_ge(prep_pool, 7)
                    for i in range(NT):
                        y = nS[:, b, P * i:P * i + P]
                        ins = split_mm(ps[0:P, 7, E * i:E * i + E], [(y, gate_h[:, :]), (y, gate_l[:, :])])
                    ins.then_inc(lg_mm, 1)
                elif step < 5:
                    pe.wait_ge(cw_done, b + 1)
                    for i in range(3):
                        ins = tp(ps[0:E, 7, P * i:P * i + P], cws[:, 3 * (step - 3) + i, :], ident[0:P, 0:P])
                    ins.then_inc(cwT_mm, 1)
                else:
                    pe.wait_ge(cw_l, 2 * b + 2)
                    for i in range(NT):
                        c = cwS[:, NP * b + P * i:NP * b + P * i + P]
                        ins = split_mm(ps[0:P, 7, C * i:C * i + C], [(c, b2_h[:, :]), (c, b2_l[:, :])])
                    ins.then_inc(b2_mm, 1)

            scores(0)
            scores(1)
            for n in range(B * NT):
                probs_up(n)
                if n + 2 < B * NT:
                    scores(n + 2)
                for b, step in PE_POST.get(n - 0.5, ()):
                    post(b, step)
                values(n)
                for b, step in PE_POST.get(n, ()):
                    post(b, step)

            def up(k):
                n, e = k // E, k % E
                b, hf = n // 2, n % 2
                x = nS[:, b, HALF * hf:HALF * hf + HALF]
                at_least(pe, gelu_done, k - 1)
                split_mm(ps[:, k % 2, 0:HALF], [(w1_h[:, e, :], x), (w1_l[:, e, :], x)]).then_inc(up_mm, 1)
                at_least(pe, gw_done, k - 1)
                mm(ps[:, 2 + k % 2, 0:HALF], picker[:, e, :], cwS[:, HALF * n:HALF * n + HALF],
                   start=True, stop=True).then_inc(cb_mm, 1)

            def down(k):
                n, e = k // E, k % E
                if e in HI_DVE[n]:
                    pe.wait_ge(gl_dve, n_dve(k + 1))
                else:
                    pe.wait_ge(gl_pool, k + 1 - n_dve(k + 1))
                if e == 0:
                    at_least(pe, y_copied, n - 1)
                w = w2_hl[:, e, :, :].rearrange("p l c -> p (l c)")
                split_mm(ps[:, 4 + n % 2, 0:HALF], [(w, gh[:, k % RH, :]), (w, gl[:, k % RH, :])],
                         start=(e == 0), stop=(e == E - 1)).then_inc(down_mm, 1)

            def y_rows(n):
                pe.wait_ge(y_copied, n + 1)
                at_least(pe, y_sum, n)
                for t in range(3):
                    ins = tp(ps[0:P, 6, 128 * t:128 * t + 128], ysb[:, n % 2, P * t:P * t + P], ident[:, :])
                ins.then_inc(yT_mm, 1)

            pe.wait_ge(s_max, B * NT)
            LAG = 5
            for k in range(KC + LAG):
                if k % (2 * E) == 0 and k < KC:
                    pe.wait_ge(cw_l, k // E + 2)
                if k == E:
                    pe.wait_ge(o_read, 2 * B)
                if k < KC:
                    up(k)
                for b, step in PE_POST.get(S0 + k, ()):
                    post(b, step)
                if k >= LAG:
                    down(k - LAG)
                if k % E == 7 and k > E and k < KC:
                    y_rows(k // E - 1)
            y_rows(KC // E - 1)


_INS = ['x', 'x_columns', 'L0_tok_W_qry', 'L0_tok_W_key', 'L0_tok_v', 'L0_tok_b', 'L0_attn_ln1_g', 'L0_attn_ln1_b',
        'L0_attn_qkv_w', 'L0_attn_qkv_b', 'L0_attn_bias_table', 'L0_attn_scale', 'L0_attn_proj_w',
        'L0_attn_proj_b', 'L0_attn_ln2_g', 'L0_attn_ln2_b', 'L0_ffn_gate_w', 'L0_ffn_gate_b', 'L0_ffn_W1',
        'L0_ffn_b1', 'L0_ffn_W2', 'L0_ffn_b2']


def kernel(**inputs):
    import numpy as _np
    import concourse.bacc as _bacc
    from concourse.bass_utils import run_bass_kernel_spmd as _run

    nc = _bacc.Bacc("TRN2", target_bir_lowering=False, num_devices=1)
    arrays, args = {}, []
    for name in _INS:
        a = _np.asarray(inputs['x' if name == 'x_columns' else name])
        if name == 'x_columns':
            a = a.transpose(0, 2, 1).reshape(B // 2, 2 * C, L)
        if name == 'L0_attn_bias_table':
            a = a[::-1]
        if name == 'L0_ffn_b1':
            a = a.T
        if name == 'L0_attn_scale':
            a = a.reshape(1, 1)
        a = _np.ascontiguousarray(a)
        arrays[f"in_{name}"] = a
        args.append(nc.dram_tensor(f"in_{name}", a.shape, mybir.dt.from_np(a.dtype), kind="ExternalInput").ap())
    args.append(nc.dram_tensor("out_0", (B, NW, C), F32, kind="ExternalOutput").ap())
    audio_tower(nc, *args)
    r = _run(nc, [arrays], core_ids=[0])
    return r.results[0]["out_0"]
```
